# Optimizing a Trainium2 kernel written in Bass

```python
import numpy as np
import jax
import jax.numpy as jnp

def _softmax(x, axis=-1):
    return jax.nn.softmax(x, axis=axis)

def _gelu(x):
    return jax.nn.gelu(x, approximate=True)

def _silu(x):
    return jax.nn.silu(x)

def _sigmoid(x):
    return jax.nn.sigmoid(x)

def _layernorm(x, axis=-1, eps=1e-05):
    m = jnp.mean(x, axis=axis, keepdims=True)
    v = jnp.var(x, axis=axis, keepdims=True)
    return (x - m) / jnp.sqrt(v + eps)

def _scatter_add(tgt, idx, src, axis=0):
    return tgt.at[idx].add(src)

def _segment_sum(src, seg, n):
    return jax.ops.segment_sum(src, seg, n)
kernel_name = 'mk_adaln_d2_jaxref_r8_ace0a3'

def setup_inputs(seed: int=0):
    np.random.seed(seed)
    _w = jnp.asarray

    def _L0_attn_setup():
        import jax, jax.numpy as jnp
        import numpy as np
        import math
        D_MODEL = 256
        D_STATE = 16
        EXPAND = 2
        D_INNER = D_MODEL * EXPAND
        DT_RANK = math.ceil(D_MODEL / 16)
        BATCH, SEQ_LEN = (2, 64)
        key = jax.random.key(seed)
        ks = jax.random.split(key, 6)
        x = jax.random.normal(ks[0], (BATCH, SEQ_LEN, D_INNER), dtype=jnp.float32)
        A_log = jnp.log(jax.random.uniform(ks[1], (D_INNER, D_STATE), minval=0.5, maxval=16.0, dtype=jnp.float32))
        D = jnp.ones((D_INNER,), dtype=jnp.float32)
        x_proj_w = 0.02 * jax.random.normal(ks[2], (DT_RANK + 2 * D_STATE, D_INNER), dtype=jnp.float32)
        dt_init_std = DT_RANK ** (-0.5)
        dt_proj_w = jax.random.uniform(ks[3], (D_INNER, DT_RANK), minval=-dt_init_std, maxval=dt_init_std, dtype=jnp.float32)
        dt = jnp.exp(jax.random.uniform(ks[4], (D_INNER,), dtype=jnp.float32) * (math.log(0.1) - math.log(0.001)) + math.log(0.001))
        dt = jnp.clip(dt, 0.0001, None)
        dt_proj_b = dt + jnp.log(-jnp.expm1(-dt))
        return {'x': x, 'A_log': A_log, 'D': D, 'x_proj_w': x_proj_w, 'dt_proj_w': dt_proj_w, 'dt_proj_b': dt_proj_b}
    _L0_attn_in = _L0_attn_setup()

    def _L0_ffn_setup():
        import jax, jax.numpy as jnp
        import numpy as np
        SCALING = 32.0 / 16.0
        key = jax.random.key(seed)
        ks = jax.random.split(key, 7)
        B, T, D, O, R, E = (4, 256, 512, 512, 16, 8)
        x = jax.random.normal(ks[0], (B, T, D), dtype=jnp.float32)
        base_W = jax.random.normal(ks[1], (O, D), dtype=jnp.float32) * D ** (-0.5)
        base_b = jax.random.normal(ks[2], (O,), dtype=jnp.float32) * 0.01
        router_W = jax.random.normal(ks[3], (2 * E - 1, D), dtype=jnp.float32) * D ** (-0.5)
        router_b = jax.random.normal(ks[4], (2 * E - 1,), dtype=jnp.float32) * 0.01
        A = jax.random.normal(ks[5], (E, R, D), dtype=jnp.float32) * D ** (-0.5)
        Bm = jax.random.normal(ks[6], (E, O, R), dtype=jnp.float32) * R ** (-0.5)
        assigned_idx = 0
        others = [i for i in range(E) if i != assigned_idx]
        expert_map = jnp.array([assigned_idx] * E + others, dtype=jnp.int32)
        return {'x': x, 'base_W': base_W, 'base_b': base_b, 'router_W': router_W, 'router_b': router_b, 'A': A, 'B': Bm, 'expert_map': expert_map}
    _L0_ffn_in = _L0_ffn_setup()
    _L0_c = _w((lambda *s: np.random.randn(*s).astype(np.float32) * 0.05)(1, 512))
    _L0_wmod = _w((lambda *s: np.random.randn(*s).astype(np.float32) * 0.05)(512, 6 * 512) * 512 ** (-0.5))

    def _L1_attn_setup():
        import jax, jax.numpy as jnp
        import numpy as np
        import math
        HIDDEN = 512
        NUM_HEADS = 32
        HEAD_DIM = HIDDEN // NUM_HEADS
        SCALE = 1.0 / HEAD_DIM

        def _alibi_slopes(n_heads: int) -> np.ndarray:
            cp2 = 2 ** math.floor(math.log2(n_heads))
            base = 2 ** (-2 ** (-(math.log2(cp2) - 3)))
            slopes = base ** np.arange(1, cp2 + 1, dtype=np.float32)
            if cp2 != n_heads:
                extra_base = 2 ** (-2 ** (-(math.log2(2 * cp2) - 3)))
                n_rem = min(cp2, n_heads - cp2)
                extra = extra_base ** np.arange(1, 1 + 2 * n_rem, 2, dtype=np.float32)
                slopes = np.concatenate([slopes, extra])
            return slopes.astype(np.float32)
        key = jax.random.key(seed)
        k1, k2, k3, k4, k5 = jax.random.split(key, 5)
        B, S = (2, 256)
        return {'hidden_states': jax.random.normal(k1, (B, S, HIDDEN), dtype=jnp.float32), 'w_attn': jax.random.normal(k2, (HIDDEN, 3 * HIDDEN), dtype=jnp.float32) * 0.02, 'b_attn': jnp.zeros((3 * HIDDEN,), dtype=jnp.float32), 'w_proj': jax.random.normal(k3, (HIDDEN, HIDDEN), dtype=jnp.float32) * 0.02, 'b_proj': jnp.zeros((HIDDEN,), dtype=jnp.float32)}
    _L1_attn_in = _L1_attn_setup()

    def _L1_ffn_setup():
        import jax, jax.numpy as jnp
        import numpy as np
        HIDDEN = 512
        INTER = 1376

        def _ternary_quantize(w):
            scale = jnp.mean(jnp.abs(w))
            return jnp.clip(jnp.round(w / scale), -1.0, 1.0) * scale
        key = jax.random.key(seed)
        kx, kg, ku, kd = jax.random.split(key, 4)
        x = jax.random.normal(kx, (2, 256, HIDDEN), dtype=jnp.float32)
        w_gate = _ternary_quantize(jax.random.normal(kg, (INTER, HIDDEN), dtype=jnp.float32) * 0.02)
        w_up = _ternary_quantize(jax.random.normal(ku, (INTER, HIDDEN), dtype=jnp.float32) * 0.02)
        w_down = _ternary_quantize(jax.random.normal(kd, (HIDDEN, INTER), dtype=jnp.float32) * 0.02)
        return {'x': x, 'w_gate': w_gate, 'w_up': w_up, 'w_down': w_down}
    _L1_ffn_in = _L1_ffn_setup()
    _L1_c = _w((lambda *s: np.random.randn(*s).astype(np.float32) * 0.05)(1, 512))
    _L1_wmod = _w((lambda *s: np.random.randn(*s).astype(np.float32) * 0.05)(512, 6 * 512) * 512 ** (-0.5))
    _d = {'L0_attn_x': _L0_attn_in['x'], 'L0_attn_A_log': _L0_attn_in['A_log'], 'L0_attn_D': _L0_attn_in['D'], 'L0_attn_x_proj_w': _L0_attn_in['x_proj_w'], 'L0_attn_dt_proj_w': _L0_attn_in['dt_proj_w'], 'L0_attn_dt_proj_b': _L0_attn_in['dt_proj_b'], 'L0_ffn_base_W': _L0_ffn_in['base_W'], 'L0_ffn_base_b': _L0_ffn_in['base_b'], 'L0_ffn_router_W': _L0_ffn_in['router_W'], 'L0_ffn_router_b': _L0_ffn_in['router_b'], 'L0_ffn_A': _L0_ffn_in['A'], 'L0_ffn_B': _L0_ffn_in['B'], 'L0_ffn_expert_map': _L0_ffn_in['expert_map'], 'L0_c': _L0_c, 'L0_wmod': _L0_wmod, 'L1_attn_w_attn': _L1_attn_in['w_attn'], 'L1_attn_b_attn': _L1_attn_in['b_attn'], 'L1_attn_w_proj': _L1_attn_in['w_proj'], 'L1_attn_b_proj': _L1_attn_in['b_proj'], 'L1_ffn_w_gate': _L1_ffn_in['w_gate'], 'L1_ffn_w_up': _L1_ffn_in['w_up'], 'L1_ffn_w_down': _L1_ffn_in['w_down'], 'L1_c': _L1_c, 'L1_wmod': _L1_wmod}
    _x0 = _d['L0_attn_x']
    _d['L0_attn_x'] = jax.random.normal(jax.random.fold_in(jax.random.key(seed), 1), (1, 1024, 512), dtype=_x0.dtype)
    del _x0
    return _d

def reference(L0_attn_x, L0_attn_A_log, L0_attn_D, L0_attn_x_proj_w, L0_attn_dt_proj_w, L0_attn_dt_proj_b, L0_ffn_base_W, L0_ffn_base_b, L0_ffn_router_W, L0_ffn_router_b, L0_ffn_A, L0_ffn_B, L0_ffn_expert_map, L0_c, L0_wmod, L1_attn_w_attn, L1_attn_b_attn, L1_attn_w_proj, L1_attn_b_proj, L1_ffn_w_gate, L1_ffn_w_up, L1_ffn_w_down, L1_c, L1_wmod):

    def _L0_attn_ref(x, A_log, D, x_proj_w, dt_proj_w, dt_proj_b):
        import jax, jax.numpy as jnp
        import numpy as np
        import math
        D_MODEL = 256
        D_STATE = 16
        EXPAND = 2
        D_INNER = D_MODEL * EXPAND
        DT_RANK = math.ceil(D_MODEL / 16)
        BATCH, SEQ_LEN = (2, 64)
        A = -jnp.exp(A_log)
        xp = jnp.einsum('bld,rd->blr', x, x_proj_w)
        dt_in = xp[..., :DT_RANK]
        B = xp[..., DT_RANK:DT_RANK + D_STATE]
        C = xp[..., DT_RANK + D_STATE:]
        dt = jax.nn.softplus(jnp.einsum('blr,dr->bld', dt_in, dt_proj_w) + dt_proj_b)
        dA = jnp.exp(dt[..., None] * A)
        dBx = dt[..., None] * B[:, :, None, :] * x[..., None]

        def step(h, inp):
            dA_t, dBx_t, C_t = inp
            h = dA_t * h + dBx_t
            y = jnp.einsum('bdn,bn->bd', h, C_t)
            return (h, y)
        h0 = jnp.zeros((x.shape[0], D_INNER, D_STATE), dtype=x.dtype)
        _, ys = jax.lax.scan(step, h0, (jnp.moveaxis(dA, 1, 0), jnp.moveaxis(dBx, 1, 0), jnp.moveaxis(C, 1, 0)))
        y = jnp.moveaxis(ys, 0, 1) + D * x
        return y

    def _L0_ffn_ref(x, base_W, base_b, router_W, router_b, A, B, expert_map):
        import jax, jax.numpy as jnp
        import numpy as np
        SCALING = 32.0 / 16.0
        E = A.shape[0]
        base_out = jnp.einsum('btd,od->bto', x, base_W) + base_b
        logits = jnp.einsum('btd,nd->btn', x, router_W) + router_b
        probs = jax.nn.softmax(logits, axis=-1)
        topk_p, topk_i = jax.lax.top_k(probs, E)
        mapped = expert_map[topk_i]
        onehot = (mapped[..., None] == jnp.arange(E)).astype(x.dtype)
        w = jnp.einsum('btk,btke->bte', topk_p, onehot)
        h = jnp.einsum('btd,erd->bter', x, A)
        lora = jnp.einsum('bter,eor->bto', h * w[..., None], B) * SCALING
        return base_out + lora

    def _L1_attn_ref(hidden_states, w_attn, b_attn, w_proj, b_proj):
        import jax, jax.numpy as jnp
        import numpy as np
        import math
        HIDDEN = 512
        NUM_HEADS = 32
        HEAD_DIM = HIDDEN // NUM_HEADS
        SCALE = 1.0 / HEAD_DIM

        def _alibi_slopes(n_heads: int) -> np.ndarray:
            cp2 = 2 ** math.floor(math.log2(n_heads))
            base = 2 ** (-2 ** (-(math.log2(cp2) - 3)))
            slopes = base ** np.arange(1, cp2 + 1, dtype=np.float32)
            if cp2 != n_heads:
                extra_base = 2 ** (-2 ** (-(math.log2(2 * cp2) - 3)))
                n_rem = min(cp2, n_heads - cp2)
                extra = extra_base ** np.arange(1, 1 + 2 * n_rem, 2, dtype=np.float32)
                slopes = np.concatenate([slopes, extra])
            return slopes.astype(np.float32)
        B, S, _ = hidden_states.shape
        H, D = (NUM_HEADS, HEAD_DIM)
        qkv = hidden_states @ w_attn + b_attn
        q, k, v = jnp.split(qkv, 3, axis=-1)
        q = q.reshape(B, S, H, D)
        k = k.reshape(B, S, H, D)
        v = v.reshape(B, S, H, D)
        scores = jnp.einsum('bqhd,bkhd->bhqk', q, k) * SCALE
        slopes = jnp.asarray(_alibi_slopes(H))
        pos = jnp.arange(S)
        rel = pos[None, :] - pos[:, None]
        bias = slopes[:, None, None] * rel[None, :, :]
        causal = rel <= 0
        scores = jnp.where(causal[None, None], scores + bias[None], -jnp.inf)
        attn = jax.nn.softmax(scores, axis=-1)
        out = jnp.einsum('bhqk,bkhd->bqhd', attn, v).reshape(B, S, HIDDEN)
        return out @ w_proj + b_proj

    def _L1_ffn_ref(x, w_gate, w_up, w_down):
        import jax, jax.numpy as jnp
        import numpy as np
        HIDDEN = 512
        INTER = 1376

        def _ternary_quantize(w):
            scale = jnp.mean(jnp.abs(w))
            return jnp.clip(jnp.round(w / scale), -1.0, 1.0) * scale
        xf = x.astype(jnp.float32) / 128.0
        gate = jnp.einsum('bsh,ih->bsi', xf, w_gate)
        up = jnp.einsum('bsh,ih->bsi', xf, w_up)
        inter = jax.nn.silu(gate) * up
        inter_q = jnp.trunc(jnp.clip(inter * 128.0, -128.0, 127.0)).astype(jnp.int8)
        down = jnp.einsum('bsi,hi->bsh', inter_q.astype(jnp.float32), w_down)
        out = jnp.trunc(jnp.clip(down * 128.0, -128.0, 127.0)).astype(jnp.int8)
        return out
    x = L0_attn_x
    mod = (_silu(L0_c) @ L0_wmod).reshape(L0_c.shape[0], 6, 1, -1)
    sa, ca, ga, sb, cb, gb = (mod[:, 0], mod[:, 1], mod[:, 2], mod[:, 3], mod[:, 4], mod[:, 5])
    ga = (2 * (ga >= 0) - 1) * jnp.maximum(jnp.abs(ga), 0.25)
    gb = (2 * (gb >= 0) - 1) * jnp.maximum(jnp.abs(gb), 0.25)
    h = _layernorm(x, axis=-1) * (1 + ca) + sa
    x = x + ga * _L0_attn_ref(h, L0_attn_A_log, L0_attn_D, L0_attn_x_proj_w, L0_attn_dt_proj_w, L0_attn_dt_proj_b)
    h = _layernorm(x, axis=-1) * (1 + cb) + sb
    x = x + gb * _L0_ffn_ref(h, L0_ffn_base_W, L0_ffn_base_b, L0_ffn_router_W, L0_ffn_router_b, L0_ffn_A, L0_ffn_B, L0_ffn_expert_map)
    mod = (_silu(L1_c) @ L1_wmod).reshape(L1_c.shape[0], 6, 1, -1)
    sa, ca, ga, sb, cb, gb = (mod[:, 0], mod[:, 1], mod[:, 2], mod[:, 3], mod[:, 4], mod[:, 5])
    ga = (2 * (ga >= 0) - 1) * jnp.maximum(jnp.abs(ga), 0.25)
    gb = (2 * (gb >= 0) - 1) * jnp.maximum(jnp.abs(gb), 0.25)
    h = _layernorm(x, axis=-1) * (1 + ca) + sa
    x = x + ga * _L1_attn_ref(h, L1_attn_w_attn, L1_attn_b_attn, L1_attn_w_proj, L1_attn_b_proj)
    h = _layernorm(x, axis=-1) * (1 + cb) + sb
    x = x + gb * _L1_ffn_ref(h, L1_ffn_w_gate, L1_ffn_w_up, L1_ffn_w_down)
    return x

_drawn_inputs = setup_inputs


def setup_inputs(seed=0):
    import zlib

    import numpy as np

    out = dict(_drawn_inputs(seed))
    spreads = {'L0_attn_D': (1.0, 0.6), 'L1_attn_b_attn': (0.0, 0.8), 'L1_attn_b_proj': (0.0, 2.0)}
    factors = {'L0_attn_A_log': 8.0,
     'L0_attn_x_proj_w': 4.905,
     'L0_attn_dt_proj_w': 8.0,
     'L0_attn_dt_proj_b': 7.357,
     'L0_ffn_base_b': 64.0,
     'L0_ffn_router_b': 200.0,
     'L1_attn_w_attn': 4.309,
     'L1_attn_w_proj': 3.452,
     'L0_ffn_router_W': 2.797}
    for name, (base, spread) in spreads.items():
        noise = np.random.default_rng([zlib.crc32(name.encode()), seed]).standard_normal(out[name].shape)
        drawn = base * np.exp(spread * noise) if base else spread * noise
        out[name] = jnp.asarray(drawn.astype(out[name].dtype))
    for name, factor in factors.items():
        out[name] = (out[name] * factor).astype(out[name].dtype)
    return out
```

```python
import math
from contextlib import ExitStack

import numpy as np

import concourse.bass as bass
from concourse import mybir

SQRT_HALF = 0.5 ** 0.5
P = 128
T, D = 1024, 512
NT, DC = T // P, D // P
HALF = 512
NS, RANK = 16, 16
E, R, NR = 8, 16, 15
NH, HD = 32, 16
GH = 4
NG = NH // GH
INTER = 1376
IC = (INTER + P - 1) // P
EPS = 1e-5
MAGIC = 12582912.0
LOW = -3e38
ATT_K = 96
ATT_R = 3
ATT_A = 24
ATT_S = ATT_K + ATT_A
ATT_ALL = ATT_S + ATT_R
PARTS_Q = (0, 0, 1, 1, 0, 2)
PARTS_K = (0, 1, 0, 1, 2, 0)

F32 = mybir.dt.float32
BF16 = mybir.dt.bfloat16
I32 = mybir.dt.int32
U16 = mybir.dt.uint16
ALU = mybir.AluOpType
ACT = mybir.ActivationFunctionType
AX = mybir.AxisListType.X

UNITS = (
    ((0, 0, 512, 0), (1, 128, 384, 512), (3, 384, 128, 896)),
    ((0, 512, 512, 0), (1, 512, 512, 512)),
    ((2, 512, 512, 0), (3, 512, 512, 512)),
    ((4, 512, 512, 0), (5, 640, 384, 512), (7, 896, 128, 896)),
    ((2, 256, 256, 0), (6, 768, 256, 256)),
)
UNIT_COLS = (1024, 1024, 1024, 1024, 512)
UNIT_AT = (0, 1024, 2048, 3072, 4096)
NU = len(UNITS)
FU = NU * GH
SPIECES = tuple((i, k0, min(512, (i + 1) * P - k0)) for i in range(NT) for k0 in (0, 512) if k0 < (i + 1) * P)
NP1 = len(SPIECES)
NPG = NP1 * GH
S_FROM, S_STEP, R_AT = 0, 3, 17


def program(nc, a, out):
    ctx = ExitStack()
    with ctx:
        KB = 1024
        base = 16512

        def at(name, kb, shape, dt=F32, off=0):
            return nc.alloc_sbuf_tensor_at(name, shape, dt, offset=base + int(kb * KB) + off)

        x_tok = at("x_tok", 0, [P, NT, D])
        xn = at("xn", 16, [P, 2, D])
        gb0 = at("gb0", 20, [P, D])
        ga1 = at("ga1", 22, [P, D])
        gb1 = at("gb1", 24, [P, D])
        small = [26 * KB]

        def tiny(name, shape, dt=F32):
            n = int(np.prod(shape[1:])) * (2 if dt == BF16 else 4)
            t = nc.alloc_sbuf_tensor_at(name, shape, dt, offset=base + small[0])
            small[0] += (n + 31) // 32 * 32
            assert small[0] <= 30 * KB
            return t

        identf = tiny("identf", [P, P])
        identb = tiny("identb", [P, P], BF16)
        sel = tiny("sel", [96, 2 * NS], BF16)
        ones = tiny("ones", [P, P])
        cc = tiny("cc", [P, 2, DC])
        ce = tiny("ce", [P, 2, DC])
        sc = tiny("sc", [P, 2, DC])
        modc = tiny("modc", [P, 2, 6, DC])
        modt = tiny("modt", [P, 2, DC])
        stats = tiny("stats", [P, NT, 6])
        mv = tiny("mv", [P, NT, 2])
        veps = tiny("veps", [P, NT])
        rstd = tiny("rstd", [P, NT])
        mhalf = tiny("mhalf", [P, NT])
        nA = tiny("nA", [P, DC * NS])
        dtb = tiny("dtb", [P, DC])
        Dp = tiny("Dp", [P, DC])
        bqk = tiny("bqk", [P, 8])
        state = tiny("state", [P, DC * NS])
        wrk = at("wrk", 30, [P, 512])
        F_AT, H_AT, WP_AT, G_AT = 32, 80, 96, 104
        wmod = at("wmod", F_AT, [P, DC, 6 * D])
        wg = at("wg", F_AT, [P, DC, INTER])
        wu = at("wu", F_AT, [P, DC, INTER], off=DC * INTER * 4)
        OT = at("OT", F_AT + 43, [P, T])
        hT = at("hT", H_AT, [P, DC, T])
        AO = at("AO", H_AT, [P, NT, D])
        wproj = at("wproj", WP_AT, [P, DC, D])
        wbase = at("wbase", G_AT, [P, DC, D])
        war = at("war", G_AT + 8, [P, DC, E * R + NR])
        wlb = at("wlb", G_AT + 8, [P, D], off=2304)
        xpw = at("xpw", G_AT + 8, [P, DC, 64], off=2304 + 2048)
        dtw = at("dtw", G_AT + 8, [RANK, D], off=2304 + 2048 + 1024)
        wattn = at("wattn", G_AT + 16, [P, DC, 3 * D])
        dtT = at("dtT", G_AT + 40, [P, DC, T])
        uT = at("uT", G_AT + 56, [P, DC, T])
        RG = G_AT + 72
        sp_log = at("sp_log", RG, [P, DC, HALF])
        sp_exp = at("sp_exp", RG + 8, [P, DC, HALF])
        sp_w = at("sp_w", RG + 16, [P, DC, HALF])
        dA = at("dA", RG, [P, DC, HALF])
        dBx = at("dBx", RG + 8, [P, DC, HALF])
        hs = at("hs", RG + 16, [P, 2, HALF])
        hC = at("hC", RG + 20, [P, 2, HALF])
        B_sb = at("B_sb", RG + 24, [P, 2, HALF])
        dtin = at("dtin", WP_AT, [RANK, T])
        BCs = at("BCs", WP_AT + 4, [96, T], BF16)
        zb = at("zb", WP_AT + 6, [P, HALF], BF16)
        mid = at("mid", WP_AT + 7, [2 * NS, HALF], BF16)
        lgt = at("lgt", RG, [P, NT, NR])
        prb = at("prb", RG + 1, [P, NT, NR])
        cmpg = at("cmpg", RG + 2, [P, NT, NR, NR])
        cmpe = at("cmpe", RG + 10, [P, NT, NR, NR])
        rank = at("rank", RG + 18, [P, NT, NR])
        wexp = at("wexp", RG + 19, [P, NT, E])
        lower = at("lower", RG + 20, [P, NR, NR])
        onehot = at("onehot", RG + 21, [P, E, NR])
        eidx = at("eidx", RG + 22, [P, E, NR])
        emapi = at("emapi", RG + 23, [P, NR], I32)
        emapf = at("emapf", RG + 23, [P, NR], F32, off=64)
        rb = at("rb", RG + 23, [P, NR], F32, off=128)
        rsum8 = at("rsum8", RG + 23, [P, 4, NT], F32, off=256)
        hw = at("hw", G_AT + 40, [P, NT, P])
        hwT = at("hwT", G_AT + 44, [P, T])
        yst = at("yst", G_AT + 48, [P, 2, D])
        bbc = at("bbc", G_AT + 52, [P, D])
        qkf = at("qkf", G_AT + 40, [P, 2, HALF])
        qkp = at("qkp", G_AT + 44, [P, 3, 3, HALF], BF16)
        vbc = at("vbc", G_AT + 54, [P, D])
        V = at("V", G_AT + 68, [P, NT, D])
        prob = at("prob", G_AT, [P, 4608])
        stack = at("stack", G_AT + 20, [P, 2, 2, GH, T], BF16)
        negm = at("negm", G_AT + 52, [P, P], BF16)
        Vp = at("Vp", G_AT + 84, [P, 2, NT, GH, 32])
        mrow = at("mrow", G_AT + 92, [P, 2, GH, NT])
        rr = at("rr", G_AT + 92, [P, GH * NT], off=256)
        rd = at("rd", G_AT + 92, [GH * NT, P], off=512)
        r3 = at("r3", G_AT + 93, [GH * NT, 3, P], BF16)
        rec = at("rec", G_AT + 94, [P, 2, 4, GH])
        AOT = at("AOT", G_AT, [P, DC, T])
        bpc = at("bpc", G_AT + 66, [P, D])
        f_e = at("f_e", G_AT, [P, 2, HALF])
        f_r = at("f_r", G_AT + 4, [P, 2, HALF])
        f_y = at("f_y", G_AT + 8, [P, 2, HALF])
        f_s = at("f_s", G_AT + 12, [P, 2, HALF])
        f_a = at("f_a", G_AT + 16, [P, 2, HALF])
        f_m = at("f_m", G_AT + 20, [P, 2, HALF])
        wd = at("wd", G_AT + 24, [P, IC, D])
        inter = at("inter", G_AT + 46, [P, IC, T], BF16)
        wdp = at("wdp", G_AT + 68, [P, 3, IC, D], BF16)

        ps = ctx.enter_context(nc.psum_tensor("ps", [P, 8, HALF], F32))
        parts_dram = nc.dram_tensor("parts_dram", (3, 2 * D, T), BF16, kind="Internal").ap()

        sems = {}

        def sem(name):
            if name not in sems:
                sems[name] = ctx.enter_context(nc.semaphore(name))
            return sems[name]

        for n in ("in_c in_x in_id in_misc in_l0 in_lf in_attn in_proj in_gu in_down wd_p0 wd_p1 wd_p2 wd_r0 wd_r1 in_att "
                  "c_exp c_silu mod_acc mod_mm mod_done negA setup "
                  "ln_ve ln_rstd ln_norm ln_tr ln_hT "
                  "xp_mm xp_dt xp_bc dt_mm sp_e sp_w sp_act sp_lo sp_dve sp_free "
                  "b_mm c_mm b_evac da_done dbx_done scan_done st_done hc_done sum_done y_done ym yt "
                  "x0 ar_mm r_soft r_exp hw_done hw_tr hw_evac f0_mm f0_y x1 x1pre bias0 "
                  "qk_mm qk_evac qk_split v_mm v_done "
                  "s_mm m_done rr_max r_part rec_done r_rdy rt_mm rt_evac st_mm exp_done pv_done ot_evac ot_tr ao_done vp_rdy vp_init "
                  "aot_tr aot_evac pj_mm pj_y x2 x2pre bias1 "
                  "g_mm f_exp f_sgn f_y0 f_out dn_mm dn_y0 dn_sgn dn_y dn_done out_dma dchain pchain achain").split():
            sem(n)
        in_wm = [[sem(f"in_wm{l}{k}") for k in range(DC)] for l in range(2)]
        qk_wr = [sem(f"qk_wr{i}") for i in range(3)]
        stk = [[sem(f"stk{i}{a_}") for a_ in range(2)] for i in range(2)]
        rrow = [sem(f"rrow{i}") for i in range(2)]
        S = sems

        block = ctx.enter_context(nc.Block())

        def half(h):
            return slice(h * HALF, (h + 1) * HALF)

        def tile(t):
            return slice(t * P, (t + 1) * P)

        def groups(eng, body):
            body(0, 0, False)
            body(1, 1, False)
            with eng.Fori(1, NG // 2 - 1) as m:
                body(m * 2, 0, False)
                body(m * 2 + 1, 1, False)
            body(NG - 2, 0, False)
            body(NG - 1, 1, True)

        def first(g):
            return isinstance(g, int) and g == 0

        def scan_turns(eng, body):
            for h in range(2):
                body(h, 0, h == 0, False)
                with eng.Fori(1, NS // 2 - 1) as m:
                    body(h, m, False, False)
                body(h, NS // 2 - 1, False, True)

        def M_of(i):
            return min(P, INTER - (i % IC) * P)

        @block.sync
        def _(sp):
            def load(dst, src, s):
                sp.dma_start(dst, src).then_inc(s, 16)

            load(cc[:], a["c"], S["in_c"])
            load(x_tok[:], a["x"], S["in_x"])
            load(identf[:], a["ident"], S["in_id"])
            for k in range(DC):
                load(wmod[:, k, :], a["wmod0"][k * P:(k + 1) * P, :], in_wm[0][k])
            misc = [(sel[:].bitcast(U16), a["sel"]), (nA[:], a["A_log"]), (dtb[:], a["dt_b"]), (Dp[:], a["D"]),
                    (bqk[:], a["b_qk"]), (identb[:].bitcast(U16), a["identb"])]
            for dst, src in misc:
                load(dst, src, S["in_misc"])
            load(xpw[:], a["xpw"].rearrange("(k p) n -> p k n", p=P), S["in_l0"])
            load(dtw[:], a["dtw"], S["in_l0"])
            load(wbase[:], a["wbase"].rearrange("(k p) n -> p k n", p=P), S["in_lf"])
            load(war[:], a["war"].rearrange("(k p) n -> p k n", p=P), S["in_lf"])
            load(wlb[:], a["wlb"], S["in_lf"])
            load(wattn[:], a["wattn"].rearrange("(k p) n -> p k n", p=P), S["in_attn"])
            sp.wait_ge(S["mod_mm"], 1)
            for k in range(DC):
                load(wmod[:, k, :], a["wmod1"][k * P:(k + 1) * P, :], in_wm[1][k])
            sp.wait_ge(S["x0"], NT)
            for dst, src in ((lower[:], a["lower"]), (eidx[:], a["eidx"]), (emapi[:], a["emap"].partition_broadcast(P)),
                             (rb[:], a["router_b"].partition_broadcast(P)), (bbc[:], a["base_b"].partition_broadcast(P))):
                load(dst, src, S["bias0"])
            sp.wait_ge(S["mod_mm"], 2)
            load(wg[:], a["wg"].rearrange("(k p) n -> p k n", p=P), S["in_gu"])
            load(wu[:], a["wu"].rearrange("(k p) n -> p k n", p=P), S["in_gu"])
            load(wproj[:], a["wproj"].rearrange("(k p) n -> p k n", p=P), S["in_proj"])
            sp.wait_ge(S["x1"], NT)
            load(vbc[:], a["b_v"].partition_broadcast(P), S["bias1"])
            load(bpc[:], a["b_proj"].partition_broadcast(P), S["bias1"])
            for i in range(16):
                sp.wait_ge(S["qk_split"], i + 1)
                ob, h = i // 2, i % 2
                for part in range(3):
                    sp.dma_start(parts_dram[part, ob * P:(ob + 1) * P, half(h)], qkp[:, i % 3, part, :]) \
                      .then_inc(qk_wr[i % 3], 16)
            for i in range(3):
                sp.wait_ge(qk_wr[i], 16 * 3 * len(range(i, 16, 3)))
            sp.wait_ge(S["v_done"], NT)
            sp.wait_ge(S["qk_evac"], 16)
            load(negm[:].bitcast(U16), a["negm"], S["in_att"])
            for s in range(2):
                for j in range(GH):
                    load(stack[ATT_K:ATT_S, s, 0, j, :].bitcast(U16), a["qconst"], S["in_att"])
                    load(stack[ATT_S:ATT_ALL, s, 1, j, :].bitcast(U16), a["kones"], S["in_att"])

            def load_stack(g, s, a_):
                pair = slice(2 * a_, 2 * a_ + 2)
                for o, order in ((0, PARTS_Q), (1, PARTS_K)):
                    for b, part in enumerate(order):
                        src = parts_dram[part, bass.ds(g * (GH * HD) + (o * D + a_ * 2 * HD), 2 * HD), :]
                        load(stack[16 * b:16 * b + 16, s, o, pair, :],
                             src.rearrange("(h d) t -> d h t", d=HD), stk[s][a_])
                load(stack[ATT_K:ATT_S, s, 1, pair, :].bitcast(U16),
                     a["alibi"][bass.ds(g * GH + 2 * a_, 2), :, :].rearrange("h r t -> r h t"), stk[s][a_])

            def load_shift(g, s):
                sp.wait_ge(S["rt_evac"], g + 1)
                for r in range(3):
                    load(stack[ATT_S + r:ATT_S + r + 1, s, 0, :, :]
                         .rearrange("o h (i c) -> o (h i) c", c=P), r3[:, r, :], rrow[s])

            load_stack(0, 0, 0)
            load_stack(0, 0, 1)
            load_stack(1, 1, 0)
            load_shift(0, 0)

            def attention(g, s, last):
                if last:
                    return
                if not (isinstance(g, int) and g == 0):
                    sp.wait_ge(S["st_mm"], g * FU)
                load_stack(g + 1, 1 - s, 1)
                if not (isinstance(g, int) and g + 2 >= NG):
                    sp.wait_ge(S["st_mm"], g * FU + FU // 2)
                    load_stack(g + 2, s, 0)
                load_shift(g + 1, 1 - s)

            groups(sp, attention)
            sp.wait_ge(S["pv_done"], NG * FU)
            sp.wait_ge(S["ao_done"], 2 * NG)
            load(wd[:, 0:IC - 1, :], a["wd"][0:(IC - 1) * P, :].rearrange("(k p) n -> p k n", p=P), S["in_down"])
            load(wd[0:INTER - (IC - 1) * P, IC - 1, :], a["wd"][(IC - 1) * P:INTER, :], S["in_down"])
            for t in range(NT):
                sp.wait_ge(S["dn_done"], t + 1)
                sp.dma_start(out[tile(t), :], x_tok[:, t, :]).then_inc(S["out_dma"], 16)
            sp.wait_ge(S["out_dma"], 16 * NT)

        @block.gpsimd
        def _(pool):
            n = [0]

            def link(ins):
                n[0] += 1
                ins.then_inc(S["pchain"], 1)
                pool.wait_ge(S["pchain"], n[0])

            pool.memset(ones[:], 1.0).then_inc(S["setup"], 1)
            pool.memset(zb[:], 0.0).then_inc(S["setup"], 1)
            pool.memset(state[:], 0.0).then_inc(S["setup"], 1)
            link(pool.memset(mhalf[:], -0.5))

            def ln_rstd(l, h):
                pool.wait_ge(S["ln_ve"], 2 * l + h + 1)
                pool.tensor_tensor(rstd[:, 4 * h:4 * h + 4], veps[:, 4 * h:4 * h + 4], mhalf[:, 0:4], ALU.pow) \
                    .then_inc(S["ln_rstd"], 1)

            def pre_add(l, s, row):
                for t in range(NT):
                    pool.wait_ge(S["ln_norm"], NT * l + t + 1)
                    pool.tensor_tensor(x_tok[:, t, :], x_tok[:, t, :], row, ALU.add).then_inc(S[s], 1)

            def add_out(sy, sx, spre):
                for t in range(NT):
                    pool.wait_ge(S[sy], t + 1)
                    pool.wait_ge(S[spre], t + 1)
                    pool.tensor_tensor(x_tok[:, t, :], x_tok[:, t, :], yst[:, t % 2, :], ALU.add) \
                        .then_inc(S[sx], 1)

            ln_rstd(0, 0)
            ln_rstd(0, 1)
            for i in range(2 * DC):
                h, c = i // DC, i % DC
                if c == 0:
                    for c_ in range(DC):
                        pool.wait_ge(S["sp_e"], DC * h + c_ + 1)
                        pool.tensor_tensor(uT[:, c_, half(h)], sp_exp[:, c_, :], uT[:, c_, half(h)], ALU.subtract) \
                            .then_inc(S["sp_lo"], 1)
                pool.wait_ge(S["sp_dve"], i + 1)
                link(pool.tensor_tensor(dtT[:, c, half(h)], dtT[:, c, half(h)], sp_log[:, c, :], ALU.add))
                pool.tensor_tensor(uT[:, c, half(h)], dtT[:, c, half(h)], hT[:, c, half(h)], ALU.mult) \
                    .then_inc(S["sp_free"], 1)
            pool.wait_ge(S["sp_free"], 2 * DC)

            def scan(h, m, first_, last):
                for o in range(2):
                    N = m * 2 + (16 * h + o)
                    pool.wait_ge(S["b_evac"], N + 1)
                    for c in range(DC):
                        if not (first_ and o == 0):
                            pool.wait_ge(S["scan_done"], N * DC + (c - 3))
                        pool.tensor_tensor(dBx[:, c, :], uT[:, c, half(h)], B_sb[:, o, :], ALU.mult) \
                            .then_inc(S["dbx_done"], 1)

            scan_turns(pool, scan)
            ln_rstd(1, 0)
            ln_rstd(1, 1)
            pool.wait_ge(S["bias0"], 16 * 5 + 1)
            pre_add(1, "x1pre", bbc[:])
            add_out("f0_y", "x1", "x1pre")
            ln_rstd(2, 0)
            ln_rstd(2, 1)
            pool.wait_ge(S["bias1"], 16 * 2 + 1)
            pre_add(2, "x2pre", bpc[:])
            pool.wait_ge(S["v_done"], NT)
            link(pool.memset(Vp[:, :, :, :, HD:32], 0.0))
            link(pool.memset(Vp[:, :, :, :, HD:HD + 1], 1.0))
            pool.wait_ge(S["in_att"], 16 * (1 + 2 * 2 * GH))
            pool.wait_ge(S["in_misc"], 16 * 6)

            def values(g, s):
                if not (isinstance(g, int) and g < 2):
                    pool.wait_ge(S["pv_done"], g * FU - FU)
                pool.tensor_copy(Vp[:, s, :, :, 0:HD],
                                 V[:, :, bass.ds(g * (GH * HD), GH * HD)]
                                 .rearrange("p t (h d) -> p t h d", d=HD)).then_inc(S["vp_rdy"], 1)

            values(0, 0)

            def attention(g, s, last):
                if last:
                    return
                values(g + 1, 1 - s)

            groups(pool, attention)
            add_out("pj_y", "x2", "x2pre")
            ln_rstd(3, 0)
            ln_rstd(3, 1)
            for i in range(IC + 1):
                for part, k in ((0, i), (1, i - 1)):
                    if 0 <= k < IC:
                        M = M_of(k)
                        pool.wait_ge(S[f"wd_p{part}"], k + 1)
                        pool.tensor_tensor(wd[0:M, k, :], wd[0:M, k, :], wdp[0:M, part, k, :], ALU.subtract) \
                            .then_inc(S[f"wd_r{part}"], 1)

        @block.scalar
        def _(act):
            n = [0]

            def link(ins):
                n[0] += 1
                ins.then_inc(S["achain"], 1)
                act.wait_ge(S["achain"], n[0])

            A_ = act.activation
            act.preload_act_table_set("natural_log_exp_and_others")
            act.wait_ge(S["in_c"], 16)
            A_(ce[:], cc[:], ACT.Exp, scale=-1.0).then_inc(S["c_exp"], 1)

            def ln_out(l, layer, jshift, jscale):
                for h in range(2):
                    act.wait_ge(S["ln_tr"], NT * l + 4 * h + 4)
                    if h == 0:
                        act.wait_ge(S["mod_done"], layer + 1)
                    for c in range(DC):
                        A_(hT[:, c, half(h)], ps[:, 4 * h + c, :], ACT.Identity,
                           scale=modc[:, layer, jscale, c:c + 1], bias=modc[:, layer, jshift, c:c + 1]) \
                            .then_inc(S["ln_hT"], 1)

            act.wait_ge(S["in_misc"], 16 * 6)
            A_(nA[:], nA[:], ACT.Exp).then_inc(S["negA"], 1)
            ln_out(0, 0, 0, 1)
            for h in range(2):
                for c in range(DC):
                    i = DC * h + c
                    act.wait_ge(S["dt_mm"], i + 1)
                    if h:
                        act.wait_ge(S["sp_free"], c + 1)
                    link(A_(sp_log[:, c, :], ps[:, 4 * h + c, :], ACT.Abs, bias=dtb[:, c:c + 1]))
                    link(A_(sp_exp[:, c, :], sp_log[:, c, :], ACT.Exp, scale=-1.0))
                    A_(uT[:, c, half(h)], sp_exp[:, c, :], ACT.Square, scale=SQRT_HALF).then_inc(S["sp_e"], 1)
                for c in range(DC):
                    act.wait_ge(S["sp_w"], DC * h + c + 1)
                    A_(sp_log[:, c, :], sp_w[:, c, :], ACT.Ln).then_inc(S["sp_act"], 1)
            act.wait_ge(S["sp_free"], 2 * DC)
            act.wait_ge(S["negA"], 2)

            def scan(h, m, first_, last):
                for o in range(2):
                    N = m * 2 + (16 * h + o)
                    act.wait_ge(S["b_mm"], N + 1)
                    if not first_:
                        act.wait_ge(S["dbx_done"], N * DC - 4)
                    A_(B_sb[:, o, :], ps[:, 6 + o, :], ACT.Copy).then_inc(S["b_evac"], 1)
                    for c in range(DC):
                        if not (first_ and o == 0):
                            act.wait_ge(S["scan_done"], N * DC + (c - 3))
                        A_(dA[:, c, :], dtT[:, c, half(h)], ACT.Exp,
                           scale=nA[:, bass.ds(m * 2 + (o + c * NS), 1)]).then_inc(S["da_done"], 1)

            scan_turns(act, scan)
            ln_out(1, 0, 3, 4)
            act.wait_ge(S["r_soft"], 1)
            A_(prb[:], lgt[:], ACT.Exp).then_inc(S["r_exp"], 1)
            for b in range(2):
                act.wait_ge(S["hw_tr"], 4 * b + 4)
                A_(hwT[:, half(b)], ps[:, b, :], ACT.Copy).then_inc(S["hw_evac"], 1)
            ln_out(2, 1, 0, 1)
            for i in range(16):
                act.wait_ge(S["qk_mm"], i + 1)
                if i >= 2:
                    act.wait_ge(S["qk_split"], i - 1)
                A_(qkf[:, i % 2, :], ps[:, i % 4, :], ACT.Identity, bias=bqk[:, i // 2:i // 2 + 1],
                   scale=1.0 / HD if i < 8 else 1.0).then_inc(S["qk_evac"], 1)

            def attention(g, s, last):
                for f in range(FU):
                    u = f % NU
                    act.wait_ge(S["st_mm"], g * FU + (f + 1))
                    if not (first(g) and f < NU):
                        act.wait_ge(S["pv_done"], g * FU + (f - NU + 1))
                    b0 = 2 + 2 * (f % 2)
                    nb = UNIT_COLS[u] // HALF
                    A_(prob[:, UNIT_AT[u]:UNIT_AT[u] + UNIT_COLS[u]].rearrange("p (b c) -> p b c", b=nb),
                       ps[:, b0:b0 + nb, :], ACT.Exp).then_inc(S["exp_done"], 1)
                act.wait_ge(S["pv_done"], g * FU + FU)
                if not first(g):
                    act.wait_ge(S["ot_tr"], g * 2)
                for b in range(2):
                    A_(OT[:, half(b)], ps[:, 6 + b, :], ACT.Copy).then_inc(S["ot_evac"], 1)

            groups(act, attention)
            for h in range(2):
                act.wait_ge(S["aot_tr"], 4 * h + 4)
                for c in range(DC):
                    A_(AOT[:, c, half(h)], ps[:, 4 * h + c, :], ACT.Copy).then_inc(S["aot_evac"], 1)
            ln_out(3, 1, 3, 4)
            for i in range(2 * IC):
                ib, s = i % IC, i % 2
                M = min(P, INTER - ib * P)
                for part in range(3):
                    k = i - part
                    if 0 <= k < IC:
                        if part == 0 and k == 0:
                            act.wait_ge(S["in_down"], 32)
                        if part:
                            act.wait_ge(S[f"wd_r{part - 1}"], k + 1)
                        A_(wdp[0:M_of(k), part, k, :], wd[0:M_of(k), k, :], ACT.Copy).then_inc(S[f"wd_p{part}"], 1)
                act.wait_ge(S["g_mm"], i + 1)
                if i >= 2:
                    act.wait_ge(S["f_y0"], i - 1)
                link(A_(f_e[0:M, s, :], ps[0:M, 2 * s, :], ACT.Exp, scale=-1.0))
                link(A_(f_e[0:M, s, :], f_e[0:M, s, :], ACT.Ln, bias=1.0))
                A_(f_e[0:M, s, :], f_e[0:M, s, :], ACT.Exp, scale=-1.0).then_inc(S["f_exp"], 1)
                act.wait_ge(S["f_y0"], i + 1)
                if i >= 2:
                    act.wait_ge(S["f_out"], i - 1)
                A_(f_s[0:M, s, :], f_y[0:M, s, :], ACT.Sign).then_inc(S["f_sgn"], 1)
            for t in range(NT):
                act.wait_ge(S["dn_y0"], t + 1)
                if t >= 2:
                    act.wait_ge(S["dn_y"], t - 1)
                A_(f_s[:, t % 2, :], f_y[:, t % 2, :], ACT.Sign).then_inc(S["dn_sgn"], 1)

        @block.tensor
        def _(pe):
            mm = pe.matmul

            def ln_transpose(l, h):
                for t in range(4 * h, 4 * h + 4):
                    pe.wait_ge(S["ln_norm"], NT * l + t + 1)
                    for c in range(DC):
                        ins = pe.transpose(ps[:, 4 * h + c, (t % 4) * P:(t % 4 + 1) * P],
                                           xn[:, t % 2, c * P:(c + 1) * P], identf[:])
                    ins.then_inc(S["ln_tr"], 1)

            def modulations(layer, cols, rows, bank):
                pe.wait_ge(S["mod_acc"], layer + 1)
                for j in cols:
                    for c in range(DC):
                        mm(ps[:, bank, j * DC + c:j * DC + c + 1], wmod[:, 0, j * D + c * P:j * D + (c + 1) * P],
                           ones[:, 0:1], start=True, stop=True)
                for r, j in enumerate(rows):
                    ins = mm(ps[:, bank + 1 + r, :], ones[:], wmod[:, 0, j * D:(j + 1) * D], start=True, stop=True)
                ins.then_inc(S["mod_mm"], 1)

            pe.wait_ge(S["in_id"], 16)
            pe.wait_ge(S["setup"], 3)
            ln_transpose(0, 0)
            modulations(0, (0, 1, 2, 3, 4), (5,), 6)
            pe.wait_ge(S["mod_done"], 1)
            ln_transpose(0, 1)
            pe.wait_ge(S["in_l0"], 32)
            for h in range(2):
                pe.wait_ge(S["ln_hT"], 4 * h + 4)
                for k in range(DC):
                    ins = mm(ps[0:64, 4 * h, :], xpw[:, k, :], hT[:, k, half(h)], start=(k == 0), stop=(k == DC - 1))
                ins.then_inc(S["xp_mm"], 1)
                pe.wait_ge(S["xp_dt"], h + 1)
                for c in range(DC):
                    mm(ps[:, 4 * h + c, :], dtw[:, c * P:(c + 1) * P], dtin[:, half(h)], start=True, stop=True) \
                        .then_inc(S["dt_mm"], 1)

            def broadcast(h, n, o, guarded):
                N = n + 16 * h
                if guarded:
                    pe.wait_ge(S["b_evac"], N - 1)
                mm(ps[:, 6 + o, :], sel[:, bass.ds(n, 1)].to_broadcast([96, P]), BCs[:, half(h)],
                   start=True, stop=True).then_inc(S["b_mm"], 1)
                if guarded:
                    pe.wait_ge(S["hc_done"], N * DC - 4)
                mm(ps[:, 4 + o, :], sel[:, bass.ds(n + NS, 1)].to_broadcast([96, P]), BCs[:, half(h)],
                   start=True, stop=True).then_inc(S["c_mm"], 1)

            def scan(h, m, first_, last):
                if isinstance(m, int) and m == 0:
                    if h == 0:
                        pe.wait_ge(S["in_misc"], 16 * 6)
                        pe.wait_ge(S["xp_bc"], 2)
                        pe.wait_ge(S["sp_dve"], 2 * DC)
                        pe.wait_ge(S["sp_act"], 2 * DC)
                    else:
                        pe.wait_ge(S["x0"], 4)
                    for c in range(DC):
                        mm(ps[:, c, :], zb[:, 0:P], zb[:], start=True, stop=False, skip_group_check=True)
                    broadcast(h, 0, 0, h > 0)
                    broadcast(h, 1, 1, h > 0)
                for o in range(2):
                    N = m * 2 + (16 * h + o)
                    for c in range(DC):
                        pe.wait_ge(S["hc_done"], N * DC + (c + 1))
                        mm(ps[:, c, :], identf[:], hC[:, c % 2, :], start=False, stop=False,
                           skip_group_check=True).then_inc(S["sum_done"], 1)
                    if not last:
                        broadcast(h, m * 2 + (2 + o), o, True)
                if last:
                    for c in range(DC):
                        ins = mm(ps[:, c, :], zb[:, 0:P], zb[:], start=False, stop=True, skip_group_check=True)
                    ins.then_inc(S["y_done"], 1)
                    pe.wait_ge(S["ym"], 4 * h + 4)
                    for t in range(4):
                        for c in range(DC):
                            ins = pe.transpose(ps[:, t, c * P:(c + 1) * P],
                                               dtT[:, c, (4 * h + t) * P:(4 * h + t + 1) * P], identf[:])
                        ins.then_inc(S["yt"], 1)

            scan_turns(pe, scan)

            pe.wait_ge(S["x0"], NT)
            ln_transpose(1, 0)
            ln_transpose(1, 1)
            pe.wait_ge(S["in_lf"], 48)
            pe.wait_ge(S["ln_hT"], 16)
            for t in range(NT):
                for k in range(DC):
                    ins = mm(ps[:, t // 2, (t % 2) * 256:(t % 2) * 256 + E * R + NR], hT[:, k, tile(t)], war[:, k, :],
                             start=(k == 0), stop=(k == DC - 1))
                ins.then_inc(S["ar_mm"], 1)

            def base_out(t):
                for k in range(DC):
                    mm(ps[:, 4 + t % 4, :], hT[:, k, tile(t)], wbase[:, k, :], start=(k == 0), stop=False)

            def lora_out(t):
                mm(ps[:, 4 + t % 4, :], hwT[:, tile(t)], wlb[:], start=False, stop=True).then_inc(S["f0_mm"], 1)

            for t in range(4):
                base_out(t)
            pe.wait_ge(S["hw_done"], 1)
            for t in range(NT):
                pe.transpose(ps[:, t // 4, (t % 4) * P:(t % 4 + 1) * P], hw[:, t, :], identf[:]) \
                    .then_inc(S["hw_tr"], 1)
            pe.wait_ge(S["hw_evac"], 2)
            for t in range(4):
                lora_out(t)
            for t in range(4, NT):
                pe.wait_ge(S["f0_y"], t - 3)
                base_out(t)
                lora_out(t)
            modulations(1, (0, 1, 3, 4), (2, 5), 1)
            pe.wait_ge(S["x1"], NT)
            pe.wait_ge(S["mod_done"], 2)
            ln_transpose(2, 0)
            ln_transpose(2, 1)
            pe.wait_ge(S["in_attn"], 16)
            pe.wait_ge(S["ln_hT"], 24)
            for i in range(16):
                if i >= 4:
                    pe.wait_ge(S["qk_evac"], i - 3)
                for k in range(DC):
                    ins = mm(ps[:, i % 4, :], wattn[:, k, (i // 2) * P:(i // 2 + 1) * P], hT[:, k, half(i % 2)],
                             start=(k == 0), stop=(k == DC - 1))
                ins.then_inc(S["qk_mm"], 1)
            for t in range(NT):
                if t >= 4:
                    pe.wait_ge(S["v_done"], t - 3)
                for k in range(DC):
                    ins = mm(ps[:, 4 + t % 4, :], hT[:, k, tile(t)], wattn[:, k, 2 * D:3 * D],
                             start=(k == 0), stop=(k == DC - 1))
                ins.then_inc(S["v_mm"], 1)

            def shift_transpose(g):
                pe.wait_ge(S["r_rdy"], g + 1)
                pe.transpose(ps[0:GH * NT, 0, 0:P], rr[:], identf[:]).then_inc(S["rt_mm"], 1)

            def stack_waits(s, g, n):
                return (g - s) * (8 * n) + 16 * n

            pe.wait_ge(S["qk_evac"], 16)
            pe.wait_ge(S["v_done"], NT)
            pe.wait_ge(S["in_att"], 16 * (1 + 2 * 2 * GH))

            def scores(g, s, p):
                j, (i, k0, w) = p // NP1, SPIECES[p % NP1]
                if p % (NPG // 2) == 0:
                    pe.wait_ge(stk[s][p // (NPG // 2)], stack_waits(s, g, 13))
                if not (first(g) and p < 2):
                    pe.wait_ge(S["m_done"], g * NPG + (p - 1))
                if p < 2 and not (isinstance(g, int) and g < 2):
                    pe.wait_ge(S["ao_done"], g * 2 - 2)
                if p == 0 and not first(g):
                    pe.wait_ge(S["rt_evac"], g)
                diag = k0 + w == (i + 1) * P
                ins = mm(ps[:, p % 2, 0:w], stack[0:ATT_S, s, 0, j, tile(i)], stack[0:ATT_S, s, 1, j, k0:k0 + w],
                         start=True, stop=not diag)
                if diag:
                    ins = mm(ps[:, p % 2, w - P:w], negm[:], identb[:], start=False, stop=True)
                ins.then_inc(S["s_mm"], 1)

            def transposed_scores(g, s, f):
                j, u = f // NU, f % NU
                if f == 0:
                    pe.wait_ge(rrow[s], stack_waits(s, g, 3))
                if not (first(g) and f < 2):
                    pe.wait_ge(S["exp_done"], g * FU + (f - 1))
                for kb, q0, w, col in UNITS[u]:
                    bank, c0 = 2 + 2 * (f % 2) + col // HALF, col % HALF
                    diag = q0 == kb * P
                    ins = mm(ps[:, bank, c0:c0 + w], stack[0:ATT_ALL, s, 1, j, tile(kb)],
                             stack[0:ATT_ALL, s, 0, j, q0:q0 + w], start=True, stop=not diag)
                    if diag:
                        ins = mm(ps[:, bank, c0:c0 + P], identb[:], negm[:], start=False, stop=True)
                ins.then_inc(S["st_mm"], 1)

            def weighted_values(g, s, f, beside=None):
                j, u = f // NU, f % NU
                if f == 0:
                    pe.wait_ge(S["vp_rdy"], g + 1)
                    if not first(g):
                        pe.wait_ge(S["ot_evac"], g * 2)
                pe.wait_ge(S["exp_done"], g * FU + (f + 1))
                for kb, q0, w, col in UNITS[u]:
                    ins = mm(ps[32 * j:32 * j + 32, 6 + q0 // HALF, q0 % HALF:q0 % HALF + w],
                             Vp[:, s, kb, j, :], prob[:, UNIT_AT[u] + col:UNIT_AT[u] + col + w],
                             start=(kb == 0), stop=(u == NU - 1), skip_group_check=True)
                    if col + w == UNIT_COLS[u]:
                        ins.then_inc(S["pv_done"], 1)
                    elif beside is not None:
                        scores(g + 1, 1 - s, beside)

            for p in range(NPG):
                scores(0, 0, p)
            shift_transpose(0)

            def attention(g, s, last):
                for f in range(FU):
                    p = (f - S_FROM) * S_STEP
                    ahead = not last and 0 <= p < NPG
                    if ahead:
                        scores(g + 1, 1 - s, p)
                    transposed_scores(g, s, f)
                    if ahead:
                        scores(g + 1, 1 - s, p + 1)
                    if f >= 2:
                        weighted_values(g, s, f - 2, p + 2 if ahead and S_STEP > 3 and len(UNITS[(f - 2) % NU]) == 2 else None)
                    if ahead:
                        if S_STEP > 3 and len(UNITS[(f - 2) % NU]) != 2:
                            scores(g + 1, 1 - s, p + 2)
                        scores(g + 1, 1 - s, p + S_STEP - 1)
                    if not last and f == R_AT:
                        shift_transpose(g + 1)
                weighted_values(g, s, FU - 2)
                weighted_values(g, s, FU - 1)
                for b in range(2):
                    pe.wait_ge(S["ot_evac"], g * 2 + (b + 1))
                    if b == 0:
                        pe.wait_ge(S["m_done"], g * NPG + ((1 if last else 2) * NPG))
                        if last:
                            pe.wait_ge(S["ao_done"], g * 2)
                    if b == 1:
                        pe.wait_ge(S["rt_evac"], g + (1 if last else 2))
                    for t in range(4):
                        ins = pe.transpose(ps[:, 1 - b, tile(t)], OT[:, (4 * b + t) * P:(4 * b + t + 1) * P], identf[:])
                    ins.then_inc(S["ot_tr"], 1)

            groups(pe, attention)
            pe.wait_ge(S["ao_done"], 2 * NG)
            for h in range(2):
                for t in range(4 * h, 4 * h + 4):
                    for c in range(DC):
                        ins = pe.transpose(ps[:, 4 * h + c, (t % 4) * P:(t % 4 + 1) * P], AO[:, t, c * P:(c + 1) * P],
                                           identf[:])
                    ins.then_inc(S["aot_tr"], 1)
            pe.wait_ge(S["in_proj"], 16)
            for t in range(NT):
                pe.wait_ge(S["aot_evac"], 4 if t < 4 else 8)
                if t >= 4:
                    pe.wait_ge(S["pj_y"], t - 3)
                for k in range(DC):
                    ins = mm(ps[:, t % 4, :], AOT[:, k, tile(t)], wproj[:, k, :], start=(k == 0), stop=(k == DC - 1))
                ins.then_inc(S["pj_mm"], 1)
            pe.wait_ge(S["x2"], NT)
            ln_transpose(3, 0)
            ln_transpose(3, 1)
            pe.wait_ge(S["in_gu"], 32)
            for i in range(2 * IC):
                h, ib, s = i // IC, i % IC, i % 2
                M = M_of(i)
                pe.wait_ge(S["ln_hT"], 28 + 4 * h)
                if i >= 2:
                    pe.wait_ge(S["f_y0"], i - 1)
                for b, w in ((0, wg), (1, wu)):
                    for k in range(DC):
                        ins = mm(ps[0:M, 2 * s + b, :], w[:, k, ib * P:ib * P + M], hT[:, k, half(h)],
                                 start=(k == 0), stop=(k == DC - 1))
                ins.then_inc(S["g_mm"], 1)
            pe.wait_ge(S["wd_p2"], IC)
            for t in range(NT):
                pe.wait_ge(S["f_out"], IC * (t // 4 + 1))
                if t >= 4:
                    pe.wait_ge(S["dn_y"], t - 3)
                for k in range(IC):
                    M = M_of(k)
                    for part in range(3):
                        ins = mm(ps[:, 4 + t % 4, :], inter[0:M, k, tile(t)], wdp[0:M, part, k, :],
                                 start=(k == 0 and part == 0), stop=(k == IC - 1 and part == 2))
                ins.then_inc(S["dn_mm"], 1)

        @block.vector
        def _(v):
            n = [0]

            def link(ins):
                n[0] += 1
                ins.then_inc(S["dchain"], 1)
                v.wait_ge(S["dchain"], n[0])

            ts, tt, stt = v.tensor_scalar, v.tensor_tensor, v.scalar_tensor_tensor

            def ln_norm(l, h):
                for t in range(4 * h, 4 * h + 4):
                    v.bn_stats(stats[:, t, :], x_tok[:, t, :]).then_inc(S["dchain"], 1)
                    n[0] += 1
                v.wait_ge(S["dchain"], n[0])
                for t in range(4 * h, 4 * h + 4):
                    v.bn_aggr(mv[:, t, :], stats[:, t, :]).then_inc(S["dchain"], 1)
                    n[0] += 1
                v.wait_ge(S["dchain"], n[0])
                ts(veps[:, 4 * h:4 * h + 4], mv[:, 4 * h:4 * h + 4, 1], EPS, None, ALU.add).then_inc(S["ln_ve"], 1)
                v.wait_ge(S["ln_rstd"], 2 * l + h + 1)
                for t in range(4 * h, 4 * h + 4):
                    if not (l == 0 and t < 2):
                        v.wait_ge(S["ln_tr"], NT * l + t - 1)
                    ts(xn[:, t % 2, :], x_tok[:, t, :], mv[:, t, 0:1], rstd[:, t:t + 1], ALU.subtract, ALU.mult) \
                        .then_inc(S["ln_norm"], 1)

            def mod_sum(layer):
                v.wait_ge(in_wm[layer][0], 16)
                link(ts(wmod[:, 0, :], wmod[:, 0, :], sc[:, layer, 0:1], None, ALU.mult))
                for k in range(1, DC):
                    v.wait_ge(in_wm[layer][k], 16)
                    ins = stt(wmod[:, 0, :], wmod[:, k, :], sc[:, layer, k:k + 1], wmod[:, 0, :], ALU.mult, ALU.add)
                    if k < DC - 1:
                        link(ins)
                ins.then_inc(S["mod_acc"], 1)

            def gate(dst, src, tmp):
                link(ts(tmp, src, 0.0, 2.0, ALU.is_ge, ALU.mult))
                link(stt(dst, tmp, 1.0, src, ALU.subtract, ALU.mult))
                link(ts(dst, dst, 0.25, None, ALU.max))
                link(stt(dst, tmp, 1.0, dst, ALU.subtract, ALU.mult))

            v.wait_ge(S["in_c"], 16)
            v.wait_ge(S["c_exp"], 1)
            link(ts(ce[:], ce[:], 1.0, None, ALU.add))
            link(v.reciprocal(ce[:], ce[:]))
            link(tt(sc[:], cc[:], ce[:], ALU.mult))
            v.wait_ge(S["in_x"], 16)
            ln_norm(0, 0)
            mod_sum(0)
            v.wait_ge(S["mod_mm"], 1)
            link(v.tensor_copy(modc[:, 0, 0:5, :], ps[:, 6, 0:20].rearrange("p (j c) -> p j c", c=DC)))
            gate(gb0[:], ps[:, 7, :], wrk[:])
            link(ts(modc[:, 0, 1, :], modc[:, 0, 1, :], 1.0, None, ALU.add))
            link(v.tensor_copy(modt[:, 0, :], modc[:, 0, 2, :]))
            gate(modc[:, 0, 2, :], modt[:, 0, :], modt[:, 1, :])
            v.wait_ge(S["negA"], 1)
            link(ts(bqk[:, 0:4], bqk[:, 0:4], 1.0 / HD, None, ALU.mult))
            ts(nA[:], nA[:], -1.0, None, ALU.mult).then_inc(S["negA"], 1)
            ts(modc[:, 0, 4, :], modc[:, 0, 4, :], 1.0, None, ALU.add).then_inc(S["mod_done"], 1)
            ln_norm(0, 1)
            v.wait_ge(S["in_misc"], 16 * 6)
            bcf = wrk[0:32, :]
            for h in range(2):
                v.wait_ge(S["xp_mm"], h + 1)
                link(v.tensor_copy(dtin[:, half(h)], ps[0:RANK, 4 * h, :]))
                v.tensor_copy(bcf, ps[32:64, 4 * h, :]).then_inc(S["xp_dt"], 1)
                v.wait_ge(S["xp_dt"], h + 1)
                link(v.tensor_copy(BCs[0:32, half(h)], bcf))
                link(tt(bcf, bcf, BCs[0:32, half(h)], ALU.subtract))
                link(v.tensor_copy(mid[:], bcf))
                link(v.tensor_copy(BCs[32:64, half(h)], mid[:]))
                link(tt(bcf, bcf, mid[:], ALU.subtract))
                v.tensor_copy(BCs[64:96, half(h)], bcf).then_inc(S["xp_bc"], 1)
                v.wait_ge(S["xp_bc"], h + 1)
                for c in range(DC):
                    v.wait_ge(S["sp_e"], DC * h + c + 1)
                    ts(sp_w[:, c, :], sp_exp[:, c, :], 1.0, None, ALU.add).then_inc(S["sp_w"], 1)
                for c in range(DC):
                    ts(dtT[:, c, half(h)], ps[:, 4 * h + c, :], dtb[:, c:c + 1], 0.0, ALU.add, ALU.max)
                    v.wait_ge(S["sp_act"], DC * h + c + 1)
                    link(stt(sp_w[:, c, :], sp_w[:, c, :], 1.0, sp_exp[:, c, :], ALU.subtract, ALU.subtract))
                    link(tt(sp_log[:, c, :], sp_log[:, c, :], sp_w[:, c, :], ALU.subtract))
                    v.wait_ge(S["sp_lo"], DC * h + c + 1)
                    link(tt(sp_log[:, c, :], sp_log[:, c, :], uT[:, c, half(h)], ALU.max))
                    tt(sp_log[:, c, :], sp_log[:, c, :], sp_exp[:, c, :], ALU.min).then_inc(S["sp_dve"], 1)
            v.wait_ge(S["sp_free"], 2 * DC)
            v.wait_ge(S["setup"], 3)

            def scan(h, m, first_, last):
                def contribution(o, c):
                    N = m * 2 + (16 * h + o)
                    v.wait_ge(S["scan_done"], N * DC + (c + 1))
                    if h == 0:
                        v.tensor_copy(state[:, bass.ds(m * 2 + (o + c * NS), 1)], hs[:, c % 2, HALF - 1:HALF]) \
                            .then_inc(S["st_done"], 1)
                    v.wait_ge(S["c_mm"], N + 1)
                    if not (first_ and o == 0 and c < 2):
                        v.wait_ge(S["sum_done"], N * DC + (c - 1))
                    tt(hC[:, c % 2, :], hs[:, c % 2, :], ps[:, 4 + o, :], ALU.mult).then_inc(S["hc_done"], 1)

                before = None
                for o in range(2):
                    N = m * 2 + (16 * h + o)
                    for c in range(DC):
                        v.wait_ge(S["da_done"], N * DC + (c + 1))
                        v.wait_ge(S["dbx_done"], N * DC + (c + 1))
                        if not (first_ and o == 0 and c < 2):
                            v.wait_ge(S["hc_done"], N * DC + (c - 1))
                        init = 0.0 if h == 0 else state[:, bass.ds(m * 2 + (o + c * NS), 1)]
                        v.tensor_tensor_scan(hs[:, c % 2, :], dA[:, c, :], dBx[:, c, :], init, ALU.mult, ALU.add) \
                            .then_inc(S["scan_done"], 1)
                        if before:
                            contribution(*before)
                        before = (o, c)
                contribution(*before)
                if last:
                    v.wait_ge(S["y_done"], h + 1)
                    for c in range(DC):
                        link(stt(dtT[:, c, half(h)], hT[:, c, half(h)], Dp[:, c:c + 1], ps[:, c, :], ALU.mult, ALU.add))
                        ts(dtT[:, c, half(h)], dtT[:, c, half(h)], modc[:, 0, 2, c:c + 1], None, ALU.mult) \
                            .then_inc(S["ym"], 1)
                    for t in range(4):
                        v.wait_ge(S["yt"], 4 * h + t + 1)
                        tt(x_tok[:, 4 * h + t, :], x_tok[:, 4 * h + t, :], ps[:, t, :], ALU.add).then_inc(S["x0"], 1)
                    if h == 0:
                        v.wait_ge(S["st_done"], DC * NS)

            scan_turns(v, scan)
            v.wait_ge(S["x0"], NT)
            ln_norm(1, 0)
            ln_norm(1, 1)
            v.wait_ge(S["bias0"], 16 * 5)
            tt(bbc[:], bbc[:], gb0[:], ALU.mult).then_inc(S["bias0"], 1)
            link(v.tensor_copy(emapf[:], emapi[:]))
            link(tt(onehot[:], eidx[:], emapf[:].unsqueeze(1).to_broadcast([P, E, NR]), ALU.is_equal))
            for b in range(4):
                v.wait_ge(S["ar_mm"], 2 * b + 2)
                link(tt(lgt[:, 2 * b:2 * b + 2, :],
                        ps[:, b, :].rearrange("p (t c) -> p t c", t=2)[:, :, E * R:E * R + NR],
                        rb[:].unsqueeze(1).to_broadcast([P, 2, NR]), ALU.add))
            mx, sm = rsum8[:, 0, :], rsum8[:, 1, :]
            link(v.reduce_max(mx, lgt[:], AX))
            tt(lgt[:], lgt[:], mx.unsqueeze(2).to_broadcast([P, NT, NR]), ALU.subtract).then_inc(S["r_soft"], 1)
            v.wait_ge(S["r_exp"], 1)
            link(v.reduce_sum(sm, prb[:], AX))
            link(v.reciprocal(sm, sm))
            link(tt(prb[:], prb[:], sm.unsqueeze(2).to_broadcast([P, NT, NR]), ALU.mult))
            for t in range(NT):
                pj = prb[:, t, :].unsqueeze(1).to_broadcast([P, NR, NR])
                pi = prb[:, t, :].unsqueeze(2).to_broadcast([P, NR, NR])
                tt(cmpg[:, t], pj, pi, ALU.is_gt).then_inc(S["dchain"], 1)
                tt(cmpe[:, t], pj, pi, ALU.is_equal).then_inc(S["dchain"], 1)
                n[0] += 2
            v.wait_ge(S["dchain"], n[0])
            low = lower[:].rearrange("p i j -> p (i j)").unsqueeze(1).to_broadcast([P, NT, NR * NR])
            flat = lambda x: x[:].rearrange("p t i j -> p t (i j)")
            link(tt(flat(cmpe), flat(cmpe), low, ALU.mult))
            link(tt(flat(cmpg), flat(cmpg), flat(cmpe), ALU.add))
            link(v.reduce_sum(rank[:], cmpg[:], AX))
            link(stt(prb[:], rank[:], float(E), prb[:], ALU.is_lt, ALU.mult))
            link(ts(prb[:], prb[:], 2.0, None, ALU.mult))
            prod = cmpg[:].rearrange("p t i j -> p (t i j)")[:, 0:NT * E * NR]
            for t in range(NT):
                tt(prod[:, t * E * NR:(t + 1) * E * NR].rearrange("p (e i) -> p e i", e=E), onehot[:],
                   prb[:, t, :].unsqueeze(1).to_broadcast([P, E, NR]), ALU.mult).then_inc(S["dchain"], 1)
                n[0] += 1
            v.wait_ge(S["dchain"], n[0])
            link(v.reduce_sum(wexp[:].rearrange("p t e -> p (t e)"), prod.rearrange("p (k i) -> p k i", i=NR), AX))
            for b in range(4):
                ins = tt(hw[:, 2 * b:2 * b + 2, :].rearrange("p t (e r) -> p t e r", r=R),
                         ps[:, b, :].rearrange("p (t c) -> p t c", t=2)[:, :, 0:E * R]
                         .rearrange("p t (e r) -> p t e r", r=R),
                         wexp[:, 2 * b:2 * b + 2, :].unsqueeze(3).to_broadcast([P, 2, E, R]), ALU.mult)
                if b < 3:
                    link(ins)
            ins.then_inc(S["hw_done"], 1)

            def gated(mmsem, ysem, xsem, bank, g):
                for t in range(NT):
                    v.wait_ge(S[mmsem], t + 1)
                    if t >= 2:
                        v.wait_ge(S[xsem], t - 1)
                    tt(yst[:, t % 2, :], ps[:, bank + t % 4, :], g[:], ALU.mult).then_inc(S[ysem], 1)

            mod_sum(1)
            gated("f0_mm", "f0_y", "x1", 4, gb0)
            v.wait_ge(S["mod_mm"], 2)
            pm = ps[:, 1, 0:24].rearrange("p (j c) -> p j c", c=DC)
            link(v.tensor_copy(modc[:, 1, 0:2, :], pm[:, 0:2, :]))
            link(v.tensor_copy(modc[:, 1, 3:5, :], pm[:, 3:5, :]))
            gate(ga1[:], ps[:, 2, :], wrk[:])
            gate(gb1[:], ps[:, 3, :], wrk[:])
            link(ts(modc[:, 1, 1, :], modc[:, 1, 1, :], 1.0, None, ALU.add))
            link(ts(modc[:, 1, 4, :], modc[:, 1, 4, :], 1.0, 1.0 / 128.0, ALU.add, ALU.mult))
            ts(modc[:, 1, 3, :], modc[:, 1, 3, :], 1.0 / 128.0, None, ALU.mult).then_inc(S["mod_done"], 1)
            v.wait_ge(S["x1"], NT)
            ln_norm(2, 0)
            ln_norm(2, 1)
            v.wait_ge(S["bias1"], 32)
            tt(bpc[:], bpc[:], ga1[:], ALU.mult).then_inc(S["bias1"], 1)
            for i in range(16):
                s, s3 = i % 2, i % 3
                v.wait_ge(S["qk_evac"], i + 1)
                if i >= 3:
                    v.wait_ge(qk_wr[s3], 48 * (i // 3))
                link(v.tensor_copy(qkp[:, s3, 0, :], qkf[:, s, :]))
                link(tt(qkf[:, s, :], qkf[:, s, :], qkp[:, s3, 0, :], ALU.subtract))
                link(v.tensor_copy(qkp[:, s3, 1, :], qkf[:, s, :]))
                tt(qkp[:, s3, 2, :], qkf[:, s, :], qkp[:, s3, 1, :], ALU.subtract).then_inc(S["qk_split"], 1)
            for t in range(NT):
                v.wait_ge(S["v_mm"], t + 1)
                tt(V[:, t, :], ps[:, 4 + t % 4, :], vbc[:], ALU.add).then_inc(S["v_done"], 1)
            v.wait_ge(S["v_done"], NT)
            v.wait_ge(qk_wr[0], 48 * 6)
            v.wait_ge(qk_wr[1], 48 * 5)
            v.wait_ge(qk_wr[2], 48 * 5)
            link(v.memset(mrow[:], LOW))

            def maxima(g, s):
                for p in range(NPG):
                    j, (i, k0, w) = p // NP1, SPIECES[p % NP1]
                    v.wait_ge(S["s_mm"], g * NPG + (p + 1))
                    v.reduce_max(mrow[:, k0 // 512, j, i:i + 1], ps[:, p % 2, 0:w], AX).then_inc(S["m_done"], 1)
                v.wait_ge(S["m_done"], g * NPG + NPG)
                flat_m = mrow[:].rearrange("p a j i -> p a (j i)")
                if not first(g):
                    v.wait_ge(S["rt_mm"], g)
                tt(rr[:], flat_m[:, 0, :], flat_m[:, 1, :], ALU.max).then_inc(S["rr_max"], 1)
                v.wait_ge(S["rr_max"], g + 1)
                ts(rr[:], rr[:], -1.0, None, ALU.mult) \
                    .then_inc(S["r_rdy"], 1)
                v.wait_ge(S["rt_mm"], g + 1)
                if not first(g):
                    v.wait_ge(rrow[1 - s], (g - 1 - (1 - s)) * 24 + 48)
                pr = ps[0:GH * NT, 0, 0:P]
                v.tensor_copy(r3[:, 0, :], pr).then_inc(S["r_part"], 1)
                v.wait_ge(S["r_part"], g * 3 + 1)
                tt(rd[:], pr, r3[:, 0, :], ALU.subtract).then_inc(S["r_part"], 1)
                v.wait_ge(S["r_part"], g * 3 + 2)
                v.tensor_copy(r3[:, 1, :], rd[:]).then_inc(S["r_part"], 1)
                v.wait_ge(S["r_part"], g * 3 + 3)
                tt(r3[:, 2, :], rd[:], r3[:, 1, :], ALU.subtract).then_inc(S["rt_evac"], 1)

            maxima(0, 0)

            def attention(g, s, last):
                if not last:
                    maxima(g + 1, 1 - s)
                for b in range(2):
                    v.wait_ge(S["ot_tr"], g * 2 + (b + 1))
                    o = ps[:, 1 - b, :].rearrange("p (t j d) -> p t j d", t=4, d=32)
                    v.reciprocal(rec[:, b, :, :], o[:, :, :, HD]).then_inc(S["rec_done"], 1)
                    v.wait_ge(S["rec_done"], g * 2 + (b + 1))
                    tt(AO[:, 4 * b:4 * b + 4, bass.ds(g * (GH * HD), GH * HD)].rearrange("p t (j d) -> p t j d", d=HD),
                       o[:, :, :, 0:HD], rec[:, b, :, :].unsqueeze(3).to_broadcast([P, 4, GH, HD]), ALU.mult) \
                        .then_inc(S["ao_done"], 1)

            groups(v, attention)
            gated("pj_mm", "pj_y", "x2", 0, ga1)
            v.wait_ge(S["x2"], NT)
            ln_norm(3, 0)
            ln_norm(3, 1)

            def trunc(y, s, M, sgn_sem, sgn_count, dst):
                link(ts(f_a[0:M, s, :].bitcast(I32), y.bitcast(I32), 0x7FFFFFFF, None, ALU.bitwise_and))
                link(ts(f_m[0:M, s, :], f_a[0:M, s, :], MAGIC, None, ALU.add))
                link(stt(f_a[0:M, s, :], f_m[0:M, s, :], MAGIC, f_a[0:M, s, :], ALU.subtract, ALU.subtract))
                link(stt(f_m[0:M, s, :], f_a[0:M, s, :], 0.0, f_m[0:M, s, :], ALU.is_gt, ALU.subtract))
                v.wait_ge(sgn_sem, sgn_count)
                return stt(dst, f_m[0:M, s, :], MAGIC, f_s[0:M, s, :], ALU.add, ALU.mult)

            for i in range(2 * IC):
                h, ib, s = i // IC, i % IC, i % 2
                M = M_of(i)
                v.wait_ge(S["f_exp"], i + 1)
                link(stt(f_r[0:M, s, :], ps[0:M, 2 * s, :], 128.0, f_e[0:M, s, :], ALU.mult, ALU.mult))
                if i >= 2:
                    v.wait_ge(S["f_sgn"], i - 1)
                link(tt(f_y[0:M, s, :], f_r[0:M, s, :], ps[0:M, 2 * s + 1, :], ALU.mult))
                ts(f_y[0:M, s, :], f_y[0:M, s, :], -128.0, 127.0, ALU.max, ALU.min).then_inc(S["f_y0"], 1)
                v.wait_ge(S["f_y0"], i + 1)
                trunc(f_y[0:M, s, :], s, M, S["f_sgn"], i + 1, inter[0:M, ib, half(h)]).then_inc(S["f_out"], 1)
            for t in range(NT):
                s = t % 2
                v.wait_ge(S["dn_mm"], t + 1)
                link(ts(f_y[:, s, :], ps[:, 4 + t % 4, :], -128.0, -128.0, ALU.mult, ALU.max))
                ts(f_y[:, s, :], f_y[:, s, :], 127.0, None, ALU.min).then_inc(S["dn_y0"], 1)
                v.wait_ge(S["dn_y0"], t + 1)
                link(trunc(f_y[:, s, :], s, P, S["dn_sgn"], t + 1, f_r[:, s, :]))
                tt(f_r[:, s, :], f_r[:, s, :], gb1[:], ALU.mult).then_inc(S["dn_y"], 1)
                v.wait_ge(S["dn_y"], t + 1)
                tt(x_tok[:, t, :], x_tok[:, t, :], f_r[:, s, :], ALU.subtract).then_inc(S["dn_done"], 1)


def bf16_bits(x):
    b = np.ascontiguousarray(x, dtype=np.float32).view(np.uint32)
    return ((b + 0x7FFF + ((b >> 16) & 1)) >> 16).astype(np.uint16)


def bf16_value(b):
    return (b.astype(np.uint32) << 16).view(np.float32)


def alibi_slopes():
    cp2 = 2 ** math.floor(math.log2(NH))
    b = 2 ** (-2 ** (-(math.log2(cp2) - 3)))
    return (b ** np.arange(1, cp2 + 1, dtype=np.float32)).astype(np.float32)


def constants():

    def three(x):
        h = bf16_bits(x)
        m = bf16_bits(x - bf16_value(h))
        return h, m, bf16_bits(x - bf16_value(h) - bf16_value(m))

    sl = alibi_slopes()
    p = np.arange(P)
    j = np.arange(T)
    qconst = np.zeros((ATT_A, T), np.float32)
    alibi = np.zeros((NH, ATT_A, T), np.uint16)
    for b in range(NT):
        qconst[3 * b:3 * b + 3, b * P:(b + 1) * P] = 1.0
        for n, part in enumerate(three(sl[:, None] * (j - (b * P + 64)).astype(np.float32)[None, :])):
            alibi[:, 3 * b + n, :] = part
    return {
        "ident": np.eye(P, dtype=np.float32), "identb": bf16_bits(np.eye(P)),
        "sel": bf16_bits(np.tile(np.eye(2 * NS), (3, 1))),
        "negm": bf16_bits(np.where(p[:, None] > p[None, :], -1e38, 0.0)),
        "qconst": bf16_bits(qconst), "kones": bf16_bits(np.ones((ATT_R, T))), "alibi": alibi,
        "lower": np.tile(np.tril(np.ones((NR, NR), np.float32), -1)[None], (P, 1, 1)),
        "eidx": np.tile(np.arange(E, dtype=np.float32)[None, :, None], (P, 1, NR)),
    }


def kernel(**inp):
    from concourse import bacc
    from concourse.bass_utils import run_bass_kernel_spmd

    c = np.ascontiguousarray
    g = {k: np.asarray(x) for k, x in inp.items()}
    cols = lambda x: c(x.reshape(-1, P).T)
    xp = g["L0_attn_x_proj_w"]
    xpw = np.zeros((D, 64), np.float32)
    xpw[:, 0:RANK] = xp[0:RANK].T
    xpw[:, 32:64] = xp[RANK:].T
    b_attn = g["L1_attn_b_attn"]
    arrays = dict(
        x=c(g["L0_attn_x"].reshape(NT, P, D).transpose(1, 0, 2)),
        c=c(np.stack([cols(g["L0_c"][0]), cols(g["L1_c"][0])], axis=1)),
        wmod0=c(g["L0_wmod"]), wmod1=c(g["L1_wmod"]),
        A_log=c(g["L0_attn_A_log"].reshape(DC, P, NS).transpose(1, 0, 2).reshape(P, DC * NS)),
        D=cols(g["L0_attn_D"]), dt_b=cols(g["L0_attn_dt_proj_b"]),
        xpw=xpw, dtw=c(g["L0_attn_dt_proj_w"].T),
        wbase=c(g["L0_ffn_base_W"].T), base_b=c(g["L0_ffn_base_b"]),
        war=c(np.concatenate([g["L0_ffn_A"].reshape(E * R, D), g["L0_ffn_router_W"]], axis=0).T),
        router_b=c(g["L0_ffn_router_b"]), emap=c(g["L0_ffn_expert_map"]),
        wlb=c(g["L0_ffn_B"].transpose(0, 2, 1).reshape(E * R, D)),
        wattn=c(g["L1_attn_w_attn"]), b_qk=cols(b_attn[0:2 * D]), b_v=c(b_attn[2 * D:]),
        wproj=c(g["L1_attn_w_proj"]), b_proj=c(g["L1_attn_b_proj"]),
        wg=c(g["L1_ffn_w_gate"].T), wu=c(g["L1_ffn_w_up"].T), wd=c(g["L1_ffn_w_down"].T),
        **constants(),
    )
    nc = bacc.Bacc("TRN2", target_bir_lowering=False, num_devices=1)
    aps = {k: nc.dram_tensor(f"in_{k}", x.shape, mybir.dt.from_np(x.dtype), kind="ExternalInput").ap()
           for k, x in arrays.items()}
    out = nc.dram_tensor("out_x", (T, D), F32, kind="ExternalOutput").ap()
    program(nc, aps, out)
    r = run_bass_kernel_spmd(nc, [{f"in_{k}": x for k, x in arrays.items()}], core_ids=[0])
    return r.results[0]["out_x"].reshape(1, T, D)
```

```python
import math
from contextlib import ExitStack

import numpy as np

import concourse.bass as bass
from concourse import mybir

SQRT_HALF = 0.5 ** 0.5
P = 128
T, D = 1024, 512
NT, DC = T // P, D // P
HALF = 512
NS, RANK = 16, 16
E, R, NR = 8, 16, 15
NH, HD = 32, 16
GH = 4
NG = NH // GH
INTER = 1376
IC = (INTER + P - 1) // P
EPS = 1e-5
QK_ORDER = (0, 4, 1, 5, 2, 6, 3, 7)
QK_FIRST = 2
F_EARLY = 2
V_FIRST = 3
MAGIC = 12582912.0
LOW = -3e38
ATT_K = 96
ATT_R = 3
ATT_A = 24
ATT_S = ATT_K + ATT_A
ATT_ALL = ATT_S + ATT_R
PARTS_Q = (0, 0, 1, 1, 0, 2)
PARTS_K = (0, 1, 0, 1, 2, 0)

F32 = mybir.dt.float32
BF16 = mybir.dt.bfloat16
I32 = mybir.dt.int32
U16 = mybir.dt.uint16
ALU = mybir.AluOpType
ACT = mybir.ActivationFunctionType
AX = mybir.AxisListType.X

UNITS = (
    ((0, 0, 512, 0), (1, 128, 384, 512), (3, 384, 128, 896)),
    ((0, 512, 512, 0), (1, 512, 512, 512)),
    ((2, 512, 512, 0), (3, 512, 512, 512)),
    ((4, 512, 512, 0), (5, 640, 384, 512), (7, 896, 128, 896)),
    ((2, 256, 256, 0), (6, 768, 256, 256)),
)
UNIT_COLS = (1024, 1024, 1024, 1024, 512)
NU = len(UNITS)
FU = NU * GH
SPIECES = tuple((i, k0, min(512, (i + 1) * P - k0)) for i in range(NT) for k0 in (0, 512) if k0 < (i + 1) * P)
NP1 = len(SPIECES)
NPG = NP1 * GH
S_FROM, S_STEP, R_AT = 3, 4, 16


def program(nc, a, out):
    ctx = ExitStack()
    with ctx:
        KB = 1024
        base = 16512

        def at(name, kb, shape, dt=F32, off=0):
            return nc.alloc_sbuf_tensor_at(name, shape, dt, offset=base + int(kb * KB) + off)

        x_tok = at("x_tok", 0, [P, NT, D])
        xn = at("xn", 16, [P, 2, D])
        gb0 = at("gb0", 20, [P, D])
        ga1 = at("ga1", 22, [P, D])
        gb1 = at("gb1", 24, [P, D])
        small = [26 * KB]

        def tiny(name, shape, dt=F32):
            n = int(np.prod(shape[1:])) * (2 if dt == BF16 else 4)
            t = nc.alloc_sbuf_tensor_at(name, shape, dt, offset=base + small[0])
            small[0] += (n + 31) // 32 * 32
            assert small[0] <= 30 * KB
            return t

        identf = tiny("identf", [P, P])
        identb = tiny("identb", [P, P], BF16)
        sel = tiny("sel", [96, 2 * NS], BF16)
        ones = tiny("ones", [P, P])
        cc = tiny("cc", [P, 2, DC])
        ce = tiny("ce", [P, 2, DC])
        sc = tiny("sc", [P, 2, DC])
        modc = tiny("modc", [P, 2, 6, DC])
        modt = tiny("modt", [P, 2, DC])
        stats = tiny("stats", [P, NT, 6])
        mv = tiny("mv", [P, NT, 2])
        veps = tiny("veps", [P, NT])
        rstd = tiny("rstd", [P, NT])
        mhalf = tiny("mhalf", [P, NT])
        nA = tiny("nA", [P, DC * NS])
        dtb = tiny("dtb", [P, DC])
        Dp = tiny("Dp", [P, DC])
        bqk = tiny("bqk", [P, 8])
        state = tiny("state", [P, DC * NS])
        wrk = at("wrk", 30, [P, 512])
        F_AT, H_AT, WP_AT, G_AT = 32, 80, 96, 104
        wmod = at("wmod", F_AT, [P, DC, 6 * D])
        wg = at("wg", F_AT, [P, DC, INTER])
        wu = at("wu", F_AT, [P, DC, INTER], off=DC * INTER * 4)
        OT = at("OT", F_AT + 43, [P, T])
        hT = at("hT", H_AT, [P, DC, T])
        AO = at("AO", H_AT, [P, NT, D])
        wproj = at("wproj", WP_AT, [P, DC, D])
        wbase = at("wbase", G_AT, [P, DC, D])
        war = at("war", G_AT + 8, [P, DC, E * R + NR])
        wlb = at("wlb", G_AT + 8, [P, D], off=2304)
        xpw = at("xpw", G_AT + 8, [P, DC, 64], off=2304 + 2048)
        dtw = at("dtw", G_AT + 8, [RANK, D], off=2304 + 2048 + 1024)
        wattn = at("wattn", G_AT + 16, [P, DC, 3 * D])
        dtT = at("dtT", G_AT + 40, [P, DC, T])
        uT = at("uT", G_AT + 56, [P, DC, T])
        RG = G_AT + 72
        sp_log = at("sp_log", RG, [P, DC, HALF])
        sp_exp = at("sp_exp", RG + 8, [P, DC, HALF])
        sp_w = at("sp_w", RG + 16, [P, DC, HALF])
        dA = at("dA", RG, [P, DC, HALF])
        dBx = at("dBx", RG + 8, [P, DC, HALF])
        hs = at("hs", RG + 16, [P, 2, HALF])
        hC = at("hC", RG + 20, [P, 2, HALF])
        B_sb = at("B_sb", RG + 24, [P, 2, HALF])
        dtin = at("dtin", RG + 24, [RANK, T])
        BCs = at("BCs", WP_AT + 4, [96, T], BF16)
        zb = at("zb", WP_AT + 6, [P, HALF], BF16)
        mid = at("mid", 16, [2 * NS, T], BF16)
        bcf = at("bcf", WP_AT, [2 * NS, T])
        lgt = at("lgt", RG, [P, NT, NR])
        prb = at("prb", RG + 1, [P, NT, NR])
        cmpg = at("cmpg", RG + 2, [P, NT, NR, NR])
        cmpe = at("cmpe", RG + 10, [P, NT, NR, NR])
        rank = at("rank", RG + 18, [P, NT, NR])
        wexp = at("wexp", RG + 19, [P, NT, E])
        lower = at("lower", RG + 20, [P, NR, NR])
        onehot = at("onehot", RG + 21, [P, E, NR])
        eidx = at("eidx", RG + 22, [P, E, NR])
        emapi = at("emapi", RG + 23, [P, NR], I32)
        emapf = at("emapf", RG + 23, [P, NR], F32, off=64)
        rb = at("rb", RG + 23, [P, NR], F32, off=128)
        rsum8 = at("rsum8", RG + 23, [P, 4, NT], F32, off=256)
        hw = at("hw", G_AT + 40, [P, NT, P])
        hwT = at("hwT", G_AT + 44, [P, T])
        yst = at("yst", G_AT + 48, [P, 2, D])
        bbc = at("bbc", G_AT + 52, [P, D])
        qkf = at("qkf", G_AT + 40, [P, 2, HALF])
        qkp = at("qkp", G_AT + 44, [P, 3, 3, HALF], BF16)
        vbc = at("vbc", 16, [P, D])
        V = at("V", G_AT + 86, [P, NT, D])
        prob = at("prob", G_AT, [P, 2, GH, 2 * HALF])
        stack = at("stack", G_AT + 54, [P, 2, 2, GH, T], BF16)
        negm = at("negm", G_AT + 102, [P, P], BF16)
        Vp = at("Vp", G_AT + 40, [P, 2, NT, GH, 32])
        mrow = at("mrow", 30, [P, 2, GH, NT])
        rr = at("rr", 30, [P, GH * NT], off=256)
        rd = at("rd", 30, [GH * NT, P], off=512)
        r3 = at("r3", 31, [GH * NT, 3, P], BF16)
        rec = at("rec", 30, [P, 2, 4, GH], off=384)
        AOT = at("AOT", G_AT, [P, DC, T])
        bpc = at("bpc", 18, [P, D])
        f_e = at("f_e", G_AT, [P, 2, HALF])
        f_r = at("f_r", G_AT + 4, [P, 2, HALF])
        f_y = at("f_y", G_AT + 8, [P, 2, HALF])
        f_s = at("f_s", G_AT + 12, [P, 2, HALF])
        f_a = at("f_a", G_AT + 16, [P, 2, HALF])
        f_m = at("f_m", G_AT + 20, [P, 2, HALF])
        wd = at("wd", G_AT + 24, [P, IC, D])
        inter = at("inter", G_AT + 46, [P, IC, T], BF16)
        wdp = at("wdp", G_AT + 68, [P, 3, IC, D], BF16)

        ps = ctx.enter_context(nc.psum_tensor("ps", [P, 8, HALF], F32))
        parts_dram = nc.dram_tensor("parts_dram", (3, 2 * D, T), BF16, kind="Internal").ap()

        sems = {}

        def sem(name):
            if name not in sems:
                sems[name] = ctx.enter_context(nc.semaphore(name))
            return sems[name]

        for n in ("in_c in_x in_id in_misc in_l0 in_lf in_attn in_proj in_gu in_down wd_p0 wd_p1 wd_p2 wd_r0 wd_r1 in_att "
                  "c_exp mod_acc mod_prod mod_mm mod_done mod_rest negA setup "
                  "ln_ve ln_rstd ln_norm ln_tr ln_hT "
                  "xp_mm xp_dt xp_bc dt_mm sp_e sp_w sp_act sp_lo sp_dve sp_free "
                  "b_mm c_mm b_evac da_done dbx_done scan_done st_done hc_done sum_done y_done ym yt "
                  "x0 ar_mm r_soft r_exp hw_done hw_tr hw_evac f0_mm f0_y x1 x1pre bias0 "
                  "qk_mm qk_evac qk_split v_mm v_done "
                  "s_mm m_done rr_max r_part rec_done r_rdy rt_mm rt_evac st_mm exp_done pv_done ot_evac ot_tr ao_done vp_rdy "
                  "aot_tr aot_evac pj_mm pj_y x2 x2pre bias1 "
                  "g_mm f_exp f_sgn f_y0 f_out dn_mm dn_y0 dn_sgn dn_y dn_done out_dma dchain pchain achain").split():
            sem(n)
        in_wm = [[sem(f"in_wm{l}{k}") for k in range(DC)] for l in range(2)]
        qk_wr = [sem(f"qk_wr{i}") for i in range(3)]
        stk = [[sem(f"stk{i}{a_}") for a_ in range(2)] for i in range(2)]
        rrow = [sem(f"rrow{i}") for i in range(2)]
        S = sems

        block = ctx.enter_context(nc.Block())

        def half(h):
            return slice(h * HALF, (h + 1) * HALF)

        def tile(t):
            return slice(t * P, (t + 1) * P)

        def groups(eng, body):
            body(0, 0, False)
            body(1, 1, False)
            with eng.Fori(1, NG // 2 - 1) as m:
                body(m * 2, 0, False)
                body(m * 2 + 1, 1, False)
            body(NG - 2, 0, False)
            body(NG - 1, 1, True)

        def first(g):
            return isinstance(g, int) and g == 0

        def score_pieces(t, k):
            return max(0, NPG * ((t - V_FIRST) * DC + k + 1) // ((NT - V_FIRST) * DC))

        def scan_turns(eng, body):
            for h in range(2):
                body(h, 0, h == 0, False)
                with eng.Fori(1, NS // 2 - 1) as m:
                    body(h, m, False, False)
                body(h, NS // 2 - 1, False, True)

        def M_of(i):
            return min(P, INTER - (i % IC) * P)

        @block.sync
        def _(sp):
            def load(dst, src, s):
                sp.dma_start(dst, src).then_inc(s, 16)

            load(cc[:], a["c"], S["in_c"])
            load(x_tok[:], a["x"], S["in_x"])
            load(identf[:], a["ident"], S["in_id"])
            for k in range(DC):
                load(wmod[:, k, :], a["wmod0"][k * P:(k + 1) * P, :], in_wm[0][k])
            misc = [(sel[:].bitcast(U16), a["sel"]), (nA[:], a["A_log"]), (dtb[:], a["dt_b"]), (Dp[:], a["D"]),
                    (bqk[:], a["b_qk"]), (identb[:].bitcast(U16), a["identb"])]
            for dst, src in misc:
                load(dst, src, S["in_misc"])
            load(xpw[:], a["xpw"].rearrange("(k p) n -> p k n", p=P), S["in_l0"])
            load(dtw[:], a["dtw"], S["in_l0"])
            load(wbase[:], a["wbase"].rearrange("(k p) n -> p k n", p=P), S["in_lf"])
            load(war[:], a["war"].rearrange("(k p) n -> p k n", p=P), S["in_lf"])
            load(wlb[:], a["wlb"], S["in_lf"])
            load(wattn[:], a["wattn"].rearrange("(k p) n -> p k n", p=P), S["in_attn"])
            sp.wait_ge(S["mod_mm"], 2)
            for k in range(DC):
                load(wmod[:, k, :], a["wmod1"][k * P:(k + 1) * P, :], in_wm[1][k])
            sp.wait_ge(S["x0"], NT)
            for dst, src in ((lower[:], a["lower"]), (eidx[:], a["eidx"]), (emapi[:], a["emap"].partition_broadcast(P)),
                             (rb[:], a["router_b"].partition_broadcast(P)), (bbc[:], a["base_b"].partition_broadcast(P))):
                load(dst, src, S["bias0"])
            sp.wait_ge(S["mod_mm"], 3)
            load(wg[:], a["wg"].rearrange("(k p) n -> p k n", p=P), S["in_gu"])
            load(wu[:], a["wu"].rearrange("(k p) n -> p k n", p=P), S["in_gu"])
            load(wproj[:], a["wproj"].rearrange("(k p) n -> p k n", p=P), S["in_proj"])
            sp.wait_ge(S["x1"], NT)
            load(negm[:].bitcast(U16), a["negm"], S["in_att"])
            for s in range(2):
                for j in range(GH):
                    load(stack[ATT_K:ATT_S, s, 0, j, :].bitcast(U16), a["qconst"], S["in_att"])
                    load(stack[ATT_S:ATT_ALL, s, 1, j, :].bitcast(U16), a["kones"], S["in_att"])
            sp.wait_ge(S["ln_tr"], 3 * NT)
            load(vbc[:], a["b_v"].partition_broadcast(P), S["bias1"])
            load(bpc[:], a["b_proj"].partition_broadcast(P), S["bias1"])

            def load_stack(g, s, a_):
                pair = slice(2 * a_, 2 * a_ + 2)
                for o, order in ((0, PARTS_Q), (1, PARTS_K)):
                    for b, part in enumerate(order):
                        src = parts_dram[part, bass.ds(g * (GH * HD) + (o * D + a_ * 2 * HD), 2 * HD), :]
                        load(stack[16 * b:16 * b + 16, s, o, pair, :],
                             src.rearrange("(h d) t -> d h t", d=HD), stk[s][a_])
                load(stack[ATT_K:ATT_S, s, 1, pair, :].bitcast(U16),
                     a["alibi"][bass.ds(g * GH + 2 * a_, 2), :, :].rearrange("h r t -> r h t"), stk[s][a_])

            for i in range(16):
                if i == 12:
                    for r in range(3):
                        sp.wait_ge(qk_wr[r], 48 * 4)
                    load_stack(0, 0, 0)
                    load_stack(0, 0, 1)
                sp.wait_ge(S["qk_split"], i + 1)
                ob, h = QK_ORDER[i % 8], i // 8
                for part in range(3):
                    sp.dma_start(parts_dram[part, ob * P:(ob + 1) * P, half(h)], qkp[:, i % 3, part, :]) \
                      .then_inc(qk_wr[i % 3], 16)
            for i in range(3):
                sp.wait_ge(qk_wr[i], 16 * 3 * len(range(i, 16, 3)))

            def load_shift(g, s):
                sp.wait_ge(S["rt_evac"], g + 1)
                for r in range(3):
                    load(stack[ATT_S + r:ATT_S + r + 1, s, 0, :, :]
                         .rearrange("o h (i c) -> o (h i) c", c=P), r3[:, r, :], rrow[s])

            load_shift(0, 0)

            def attention(g, s, last):
                if last:
                    return
                if not (isinstance(g, int) and g == 0):
                    sp.wait_ge(S["st_mm"], g * FU)
                load_stack(g + 1, 1 - s, 0)
                load_stack(g + 1, 1 - s, 1)
                load_shift(g + 1, 1 - s)

            groups(sp, attention)
            sp.wait_ge(S["pv_done"], NG * NU)
            sp.wait_ge(S["ao_done"], 2 * NG)
            load(wd[:, 0:IC - 1, :], a["wd"][0:(IC - 1) * P, :].rearrange("(k p) n -> p k n", p=P), S["in_down"])
            load(wd[0:INTER - (IC - 1) * P, IC - 1, :], a["wd"][(IC - 1) * P:INTER, :], S["in_down"])
            for t in range(NT):
                sp.wait_ge(S["dn_done"], t + 1)
                sp.dma_start(out[tile(t), :], x_tok[:, t, :]).then_inc(S["out_dma"], 16)
            sp.wait_ge(S["out_dma"], 16 * NT)

        @block.gpsimd
        def _(pool):
            n = [0]

            def link(ins):
                n[0] += 1
                ins.then_inc(S["pchain"], 1)
                pool.wait_ge(S["pchain"], n[0])

            pool.memset(ones[:], 1.0).then_inc(S["setup"], 1)
            pool.memset(zb[:], 0.0).then_inc(S["setup"], 1)
            pool.memset(state[:], 0.0).then_inc(S["setup"], 1)
            link(pool.memset(mhalf[:], -0.5))

            def ln_rstd(l, h):
                pool.wait_ge(S["ln_ve"], 2 * l + h + 1)
                pool.tensor_tensor(rstd[:, 4 * h:4 * h + 4], veps[:, 4 * h:4 * h + 4], mhalf[:, 0:4], ALU.pow) \
                    .then_inc(S["ln_rstd"], 1)

            def pre_add(l, s, row):
                for t in range(NT):
                    pool.wait_ge(S["ln_norm"], NT * l + t + 1)
                    pool.tensor_tensor(x_tok[:, t, :], x_tok[:, t, :], row, ALU.add).then_inc(S[s], 1)

            ln_rstd(0, 0)
            ln_rstd(0, 1)
            for i in range(2 * DC):
                h, c = i // DC, i % DC
                if c == 0:
                    for c_ in range(DC):
                        pool.wait_ge(S["sp_e"], DC * h + c_ + 1)
                        pool.tensor_tensor(uT[:, c_, half(h)], sp_exp[:, c_, :], uT[:, c_, half(h)], ALU.subtract) \
                            .then_inc(S["sp_lo"], 1)
                pool.wait_ge(S["sp_dve"], i + 1)
                link(pool.tensor_tensor(dtT[:, c, half(h)], dtT[:, c, half(h)], sp_log[:, c, :], ALU.add))
                pool.tensor_tensor(uT[:, c, half(h)], dtT[:, c, half(h)], hT[:, c, half(h)], ALU.mult) \
                    .then_inc(S["sp_free"], 1)
            pool.wait_ge(S["sp_free"], 2 * DC)

            def scan(h, m, first_, last):
                for o in range(2):
                    N = m * 2 + (16 * h + o)
                    pool.wait_ge(S["b_evac"], N + 1)
                    for c in range(DC):
                        if not (first_ and o == 0):
                            pool.wait_ge(S["scan_done"], N * DC + (c - 3))
                        pool.tensor_tensor(dBx[:, c, :], uT[:, c, half(h)], B_sb[:, o, :], ALU.mult) \
                            .then_inc(S["dbx_done"], 1)

            scan_turns(pool, scan)
            ln_rstd(1, 0)
            ln_rstd(1, 1)
            pool.wait_ge(S["bias0"], 16 * 5 + 1)
            pre_add(1, "x1pre", bbc[:])
            pool.wait_ge(S["mod_prod"], 2)
            link(pool.tensor_tensor(wmod[:, 0, :], wmod[:, 0, :], wmod[:, 1, :], ALU.add))
            pool.wait_ge(S["mod_prod"], DC)
            link(pool.tensor_tensor(wmod[:, 2, :], wmod[:, 2, :], wmod[:, 3, :], ALU.add))
            pool.tensor_tensor(wmod[:, 0, :], wmod[:, 0, :], wmod[:, 2, :], ALU.add).then_inc(S["mod_acc"], 1)
            ln_rstd(2, 0)
            ln_rstd(2, 1)
            pool.wait_ge(S["bias1"], 16 * 2 + 1)
            pre_add(2, "x2pre", bpc[:])
            pool.wait_ge(S["v_done"], NT)
            for i in range(3):
                pool.wait_ge(qk_wr[i], 16 * 3 * len(range(i, 16, 3)))
            link(pool.memset(Vp[:, :, :, :, HD:32], 0.0))
            link(pool.memset(Vp[:, :, :, :, HD:HD + 1], 1.0))
            pool.wait_ge(S["in_att"], 16 * (1 + 2 * 2 * GH))
            pool.wait_ge(S["in_misc"], 16 * 6)

            def values(g, s):
                if not (isinstance(g, int) and g < 2):
                    pool.wait_ge(S["pv_done"], g * NU - NU)
                pool.tensor_copy(Vp[:, s, :, :, 0:HD],
                                 V[:, :, bass.ds(g * (GH * HD), GH * HD)]
                                 .rearrange("p t (h d) -> p t h d", d=HD)).then_inc(S["vp_rdy"], 1)

            values(0, 0)

            def attention(g, s, last):
                if last:
                    return
                values(g + 1, 1 - s)

            groups(pool, attention)
            ln_rstd(3, 0)
            ln_rstd(3, 1)
            for i in range(IC + 1):
                for part, k in ((0, i), (1, i - 1)):
                    if 0 <= k < IC:
                        M = M_of(k)
                        pool.wait_ge(S[f"wd_p{part}"], k + 1)
                        pool.tensor_tensor(wd[0:M, k, :], wd[0:M, k, :], wdp[0:M, part, k, :], ALU.subtract) \
                            .then_inc(S[f"wd_r{part}"], 1)

        @block.scalar
        def _(act):
            n = [0]

            def link(ins):
                n[0] += 1
                ins.then_inc(S["achain"], 1)
                act.wait_ge(S["achain"], n[0])

            A_ = act.activation
            act.preload_act_table_set("natural_log_exp_and_others")
            act.wait_ge(S["in_c"], 16)
            A_(ce[:], cc[:], ACT.Exp, scale=-1.0).then_inc(S["c_exp"], 1)

            def ln_out(l, layer, jshift, jscale, halves=(0, 1)):
                for h in halves:
                    act.wait_ge(S["ln_tr"], NT * l + 4 * h + 4)
                    if h == 0:
                        act.wait_ge(S["mod_done"], layer + 1)
                    for c in range(DC):
                        A_(hT[:, c, half(h)], ps[:, 4 * h + c, :], ACT.Identity,
                           scale=modc[:, layer, jscale, c:c + 1], bias=modc[:, layer, jshift, c:c + 1]) \
                            .then_inc(S["ln_hT"], 1)

            act.wait_ge(S["in_misc"], 16 * 6)
            A_(nA[:], nA[:], ACT.Exp).then_inc(S["negA"], 1)
            ln_out(0, 0, 0, 1)
            for h in range(2):
                for c in range(DC):
                    i = DC * h + c
                    act.wait_ge(S["dt_mm"], i + 1)
                    if h:
                        act.wait_ge(S["sp_free"], c + 1)
                    link(A_(sp_log[:, c, :], ps[:, 4 * h + c, :], ACT.Abs, bias=dtb[:, c:c + 1]))
                    link(A_(sp_exp[:, c, :], sp_log[:, c, :], ACT.Exp, scale=-1.0))
                    A_(uT[:, c, half(h)], sp_exp[:, c, :], ACT.Square, scale=SQRT_HALF).then_inc(S["sp_e"], 1)
                for c in range(DC):
                    act.wait_ge(S["sp_w"], DC * h + c + 1)
                    A_(sp_log[:, c, :], sp_w[:, c, :], ACT.Ln).then_inc(S["sp_act"], 1)
            act.wait_ge(S["sp_free"], 2 * DC)
            act.wait_ge(S["negA"], 2)

            def scan(h, m, first_, last):
                for o in range(2):
                    N = m * 2 + (16 * h + o)
                    act.wait_ge(S["b_mm"], N + 1)
                    if not first_:
                        act.wait_ge(S["dbx_done"], N * DC - 4)
                    A_(B_sb[:, o, :], ps[:, 6 + o, :], ACT.Copy).then_inc(S["b_evac"], 1)
                    for c in range(DC):
                        if not (first_ and o == 0):
                            act.wait_ge(S["scan_done"], N * DC + (c - 3))
                        A_(dA[:, c, :], dtT[:, c, half(h)], ACT.Exp,
                           scale=nA[:, bass.ds(m * 2 + (o + c * NS), 1)]).then_inc(S["da_done"], 1)

            scan_turns(act, scan)
            ln_out(1, 0, 3, 4)
            for k in range(DC):
                act.wait_ge(in_wm[1][k], 16)
                A_(wmod[:, k, :], wmod[:, k, :], ACT.Identity, scale=sc[:, 1, k:k + 1]).then_inc(S["mod_prod"], 1)
            act.wait_ge(S["r_soft"], 1)
            A_(prb[:], lgt[:], ACT.Exp).then_inc(S["r_exp"], 1)
            for b in range(2):
                act.wait_ge(S["hw_tr"], 4 * b + 4)
                A_(hwT[:, half(b)], ps[:, b, :], ACT.Copy).then_inc(S["hw_evac"], 1)
            ln_out(2, 1, 0, 1, (0,))
            for i in range(16):
                if i == QK_FIRST:
                    ln_out(2, 1, 0, 1, (1,))
                act.wait_ge(S["qk_mm"], i + 1)
                if i >= 2:
                    act.wait_ge(S["qk_split"], i - 1)
                ob = QK_ORDER[i % 8]
                A_(qkf[:, i % 2, :], ps[:, i % 4, :], ACT.Identity, bias=bqk[:, ob:ob + 1],
                   scale=1.0 / HD if ob < DC else 1.0).then_inc(S["qk_evac"], 1)

            def exponentials(g, s, f):
                u, j = f // GH, f % GH
                act.wait_ge(S["st_mm"], g * FU + (f + 1))
                if j == 0 and not (first(g) and u < 2):
                    act.wait_ge(S["pv_done"], g * NU + (u - 1))
                b0 = 2 + 2 * (f % 2)
                nb = UNIT_COLS[u] // HALF
                A_(prob[:, (s + u) % 2, j, 0:UNIT_COLS[u]].rearrange("p (b c) -> p b c", b=nb),
                   ps[:, b0:b0 + nb, :], ACT.Exp).then_inc(S["exp_done"], 1)

            for f in range(F_EARLY):
                exponentials(0, 0, f)

            def attention(g, s, last):
                for f in range(F_EARLY, FU):
                    exponentials(g, s, f)
                if not last:
                    for f in range(F_EARLY):
                        exponentials(g + 1, 1 - s, f)
                act.wait_ge(S["pv_done"], g * NU + NU)
                if not first(g):
                    act.wait_ge(S["ot_tr"], g * 2)
                for b in range(2):
                    A_(OT[:, half(b)], ps[:, 6 + b, :], ACT.Copy).then_inc(S["ot_evac"], 1)

            groups(act, attention)
            for h in range(2):
                act.wait_ge(S["aot_tr"], 4 * h + 4)
                for c in range(DC):
                    A_(AOT[:, c, half(h)], ps[:, 4 * h + c, :], ACT.Copy).then_inc(S["aot_evac"], 1)
            ln_out(3, 1, 3, 4, (0,))
            for i in range(2 * IC):
                if i == 1:
                    ln_out(3, 1, 3, 4, (1,))
                ib, s = i % IC, i % 2
                M = min(P, INTER - ib * P)
                for part in range(3):
                    k = i - part
                    if 0 <= k < IC:
                        if part == 0 and k == 0:
                            act.wait_ge(S["in_down"], 32)
                        if part:
                            act.wait_ge(S[f"wd_r{part - 1}"], k + 1)
                        A_(wdp[0:M_of(k), part, k, :], wd[0:M_of(k), k, :], ACT.Copy).then_inc(S[f"wd_p{part}"], 1)
                act.wait_ge(S["g_mm"], i + 1)
                if i >= 2:
                    act.wait_ge(S["f_y0"], i - 1)
                link(A_(f_e[0:M, s, :], ps[0:M, 2 * s, :], ACT.Exp, scale=-1.0))
                link(A_(f_e[0:M, s, :], f_e[0:M, s, :], ACT.Ln, bias=1.0))
                A_(f_e[0:M, s, :], f_e[0:M, s, :], ACT.Exp, scale=-1.0).then_inc(S["f_exp"], 1)
                act.wait_ge(S["f_y0"], i + 1)
                if i >= 2:
                    act.wait_ge(S["f_out"], i - 1)
                A_(f_s[0:M, s, :], f_y[0:M, s, :], ACT.Sign).then_inc(S["f_sgn"], 1)
            for t in range(NT):
                act.wait_ge(S["dn_y0"], t + 1)
                if t >= 2:
                    act.wait_ge(S["dn_y"], t - 1)
                A_(f_s[:, t % 2, :], f_y[:, t % 2, :], ACT.Sign).then_inc(S["dn_sgn"], 1)

        @block.tensor
        def _(pe):
            mm = pe.matmul

            def ln_transpose(l, h):
                for t in range(4 * h, 4 * h + 4):
                    pe.wait_ge(S["ln_norm"], NT * l + t + 1)
                    for c in range(DC):
                        ins = pe.transpose(ps[:, 4 * h + c, (t % 4) * P:(t % 4 + 1) * P],
                                           xn[:, t % 2, c * P:(c + 1) * P], identf[:])
                    ins.then_inc(S["ln_tr"], 1)

            def modulations(layer, cols, rows, bank):
                pe.wait_ge(S["mod_acc"], layer + 1)
                for j in cols:
                    for c in range(DC):
                        ins = mm(ps[:, bank, j * DC + c:j * DC + c + 1], wmod[:, 0, j * D + c * P:j * D + (c + 1) * P],
                           ones[:, 0:1], start=True, stop=True)
                for r, j in enumerate(rows):
                    ins = mm(ps[:, bank + 1 + r, :], ones[:], wmod[:, 0, j * D:(j + 1) * D], start=True, stop=True)
                ins.then_inc(S["mod_mm"], 1)

            pe.wait_ge(S["in_id"], 16)
            pe.wait_ge(S["setup"], 3)
            ln_transpose(0, 0)
            modulations(0, (0, 1), (), 6)
            pe.wait_ge(S["mod_done"], 1)
            ln_transpose(0, 1)
            pe.wait_ge(S["in_l0"], 32)
            for h in range(2):
                pe.wait_ge(S["ln_hT"], 4 * h + 4)
                for k in range(DC):
                    ins = mm(ps[0:64, 4 * h, :], xpw[:, k, :], hT[:, k, half(h)], start=(k == 0), stop=(k == DC - 1))
                ins.then_inc(S["xp_mm"], 1)
                pe.wait_ge(S["xp_dt"], h + 1)
                for c in range(DC):
                    mm(ps[:, 4 * h + c, :], dtw[:, c * P:(c + 1) * P], dtin[:, half(h)], start=True, stop=True) \
                        .then_inc(S["dt_mm"], 1)
            pe.wait_ge(S["sp_dve"], 2)
            pe.wait_ge(S["sp_e"], 2)
            modulations(0, (2, 3, 4), (5,), 0)

            def broadcast(h, n, o, guarded):
                N = n + 16 * h
                if guarded:
                    pe.wait_ge(S["b_evac"], N - 1)
                mm(ps[:, 6 + o, :], sel[:, bass.ds(n, 1)].to_broadcast([96, P]), BCs[:, half(h)],
                   start=True, stop=True).then_inc(S["b_mm"], 1)
                if guarded:
                    pe.wait_ge(S["hc_done"], N * DC - 4)
                mm(ps[:, 4 + o, :], sel[:, bass.ds(n + NS, 1)].to_broadcast([96, P]), BCs[:, half(h)],
                   start=True, stop=True).then_inc(S["c_mm"], 1)

            def scan(h, m, first_, last):
                if isinstance(m, int) and m == 0:
                    if h == 0:
                        pe.wait_ge(S["in_misc"], 16 * 6)
                        pe.wait_ge(S["xp_bc"], 2)
                        pe.wait_ge(S["sp_dve"], 2 * DC)
                        pe.wait_ge(S["sp_act"], 2 * DC)
                        pe.wait_ge(S["mod_rest"], 1)
                    else:
                        pe.wait_ge(S["x0"], 4)
                    for c in range(DC):
                        mm(ps[:, c, :], zb[:, 0:P], zb[:], start=True, stop=False, skip_group_check=True)
                    broadcast(h, 0, 0, h > 0)
                    broadcast(h, 1, 1, h > 0)
                for o in range(2):
                    N = m * 2 + (16 * h + o)
                    for c in range(DC):
                        pe.wait_ge(S["hc_done"], N * DC + (c + 1))
                        mm(ps[:, c, :], identf[:], hC[:, c % 2, :], start=False, stop=False,
                           skip_group_check=True).then_inc(S["sum_done"], 1)
                    if not last:
                        broadcast(h, m * 2 + (2 + o), o, True)
                if last:
                    for c in range(DC):
                        ins = mm(ps[:, c, :], zb[:, 0:P], zb[:], start=False, stop=True, skip_group_check=True)
                    ins.then_inc(S["y_done"], 1)
                    pe.wait_ge(S["ym"], 4 * h + 4)
                    for t in range(4):
                        for c in range(DC):
                            ins = pe.transpose(ps[:, t, c * P:(c + 1) * P],
                                               dtT[:, c, (4 * h + t) * P:(4 * h + t + 1) * P], identf[:])
                        ins.then_inc(S["yt"], 1)

            scan_turns(pe, scan)

            pe.wait_ge(S["x0"], NT)
            ln_transpose(1, 0)
            ln_transpose(1, 1)
            pe.wait_ge(S["in_lf"], 48)
            pe.wait_ge(S["ln_hT"], 16)
            for t in range(NT):
                for k in range(DC):
                    ins = mm(ps[:, t // 2, (t % 2) * 256:(t % 2) * 256 + E * R + NR], hT[:, k, tile(t)], war[:, k, :],
                             start=(k == 0), stop=(k == DC - 1))
                ins.then_inc(S["ar_mm"], 1)

            def base_out(t):
                for k in range(DC):
                    mm(ps[:, 4 + t % 4, :], hT[:, k, tile(t)], wbase[:, k, :], start=(k == 0), stop=False)

            def lora_out(t):
                mm(ps[:, 4 + t % 4, :], hwT[:, tile(t)], wlb[:], start=False, stop=True).then_inc(S["f0_mm"], 1)

            for t in range(4):
                base_out(t)
            pe.wait_ge(S["hw_done"], 1)
            for t in range(NT):
                pe.transpose(ps[:, t // 4, (t % 4) * P:(t % 4 + 1) * P], hw[:, t, :], identf[:]) \
                    .then_inc(S["hw_tr"], 1)
            pe.wait_ge(S["hw_evac"], 2)
            for t in range(4):
                lora_out(t)
            modulations(1, (0, 1, 3, 4), (2, 5), 1)
            for t in range(4, NT):
                pe.wait_ge(S["f0_y"], t - 3)
                base_out(t)
                lora_out(t)
            pe.wait_ge(S["mod_done"], 2)
            ln_transpose(2, 0)
            pe.wait_ge(S["in_attn"], 16)
            for i in range(16):
                if i == QK_FIRST:
                    pe.wait_ge(S["f0_y"], NT)
                    ln_transpose(2, 1)
                ob, h = QK_ORDER[i % 8], i // 8
                pe.wait_ge(S["ln_hT"], 20 + 4 * h)
                if i >= 4:
                    pe.wait_ge(S["qk_evac"], i - 3)
                for k in range(DC):
                    ins = mm(ps[:, i % 4, :], wattn[:, k, ob * P:(ob + 1) * P], hT[:, k, half(h)],
                             start=(k == 0), stop=(k == DC - 1))
                ins.then_inc(S["qk_mm"], 1)
            def shift_transpose(g):
                pe.wait_ge(S["r_rdy"], g + 1)
                pe.transpose(ps[0:GH * NT, 0, 0:P], rr[:], identf[:]).then_inc(S["rt_mm"], 1)

            def stack_waits(s, g, n):
                return (g - s) * (8 * n) + 16 * n

            def scores(g, s, p):
                j, (i, k0, w) = p // NP1, SPIECES[p % NP1]
                if p % (NPG // 2) == 0:
                    pe.wait_ge(stk[s][p // (NPG // 2)], stack_waits(s, g, 13))
                if not (first(g) and p < 2):
                    pe.wait_ge(S["m_done"], g * NPG + (p - 1))
                if p < 2 and not (isinstance(g, int) and g < 2):
                    pe.wait_ge(S["ao_done"], g * 2 - 2)
                if p == 0 and not first(g):
                    pe.wait_ge(S["rt_evac"], g)
                diag = k0 + w == (i + 1) * P
                ins = mm(ps[:, p % 2, 0:w], stack[0:ATT_S, s, 0, j, tile(i)], stack[0:ATT_S, s, 1, j, k0:k0 + w],
                         start=True, stop=not diag)
                if diag:
                    ins = mm(ps[:, p % 2, w - P:w], negm[:], identb[:], start=False, stop=True)
                ins.then_inc(S["s_mm"], 1)

            def transposed_scores(g, s, f):
                u, j = f // GH, f % GH
                if f == 0:
                    pe.wait_ge(rrow[s], stack_waits(s, g, 3))
                if not (first(g) and f < 2):
                    pe.wait_ge(S["exp_done"], g * FU + (f - 1))
                for kb, q0, w, col in UNITS[u]:
                    bank, c0 = 2 + 2 * (f % 2) + col // HALF, col % HALF
                    diag = q0 == kb * P
                    ins = mm(ps[:, bank, c0:c0 + w], stack[0:ATT_ALL, s, 1, j, tile(kb)],
                             stack[0:ATT_ALL, s, 0, j, q0:q0 + w], start=True, stop=not diag)
                    if diag:
                        ins = mm(ps[:, bank, c0:c0 + P], identb[:], negm[:], start=False, stop=True)
                ins.then_inc(S["st_mm"], 1)

            def weighted_values(g, s, u, piece):
                if piece == 0:
                    if u == 0:
                        pe.wait_ge(S["vp_rdy"], g + 1)
                        if not first(g):
                            pe.wait_ge(S["ot_evac"], g * 2)
                    pe.wait_ge(S["exp_done"], g * FU + (u + 1) * GH)
                kb, q0, w, col = UNITS[u][piece]
                for j in range(GH):
                    ins = mm(ps[32 * j:32 * j + 32, 6 + q0 // HALF, q0 % HALF:q0 % HALF + w],
                             Vp[:, s, kb, j, :], prob[:, (s + u) % 2, j, col:col + w],
                             start=(kb == 0), stop=(u == NU - 1), skip_group_check=True)
                if piece == len(UNITS[u]) - 1:
                    ins.then_inc(S["pv_done"], 1)

            pe.wait_ge(S["qk_evac"], 16)
            pe.wait_ge(S["in_att"], 16 * (1 + 2 * 2 * GH))
            p = 0
            for t in range(NT):
                if t >= 4:
                    pe.wait_ge(S["v_done"], t - 3)
                for k in range(DC):
                    ins = mm(ps[:, 4 + t % 4, :], hT[:, k, tile(t)], wattn[:, k, 2 * D:3 * D],
                             start=(k == 0), stop=(k == DC - 1))
                    if k == DC - 1:
                        ins.then_inc(S["v_mm"], 1)
                    while p < score_pieces(t, k):
                        scores(0, 0, p)
                        p += 1
            shift_transpose(0)
            pe.wait_ge(S["v_done"], NT)
            for f in range(F_EARLY):
                transposed_scores(0, 0, f)

            def attention(g, s, last):
                for f in range(F_EARLY, FU):
                    u, j = f // GH, f % GH
                    p = (f - S_FROM) * S_STEP
                    ahead = not last and 0 <= p < NPG
                    if ahead:
                        scores(g + 1, 1 - s, p)
                    transposed_scores(g, s, f)
                    if ahead:
                        scores(g + 1, 1 - s, p + 1)
                    if u and 1 <= j <= len(UNITS[u - 1]):
                        weighted_values(g, s, u - 1, j - 1)
                    if ahead:
                        for q in range(2, S_STEP):
                            scores(g + 1, 1 - s, p + q)
                    if not last and f == R_AT:
                        shift_transpose(g + 1)
                if not last:
                    for f in range(F_EARLY):
                        transposed_scores(g + 1, 1 - s, f)
                for piece in range(len(UNITS[NU - 1])):
                    weighted_values(g, s, NU - 1, piece)
                for b in range(2):
                    pe.wait_ge(S["ot_evac"], g * 2 + (b + 1))
                    if b == 0:
                        pe.wait_ge(S["m_done"], g * NPG + ((1 if last else 2) * NPG))
                        if last:
                            pe.wait_ge(S["ao_done"], g * 2)
                    if b == 1:
                        pe.wait_ge(S["rt_evac"], g + (1 if last else 2))
                    for t in range(4):
                        ins = pe.transpose(ps[:, 1 - b, tile(t)], OT[:, (4 * b + t) * P:(4 * b + t + 1) * P], identf[:])
                    ins.then_inc(S["ot_tr"], 1)

            groups(pe, attention)
            pe.wait_ge(S["ao_done"], 2 * NG)
            for h in range(2):
                for t in range(4 * h, 4 * h + 4):
                    for c in range(DC):
                        ins = pe.transpose(ps[:, 4 * h + c, (t % 4) * P:(t % 4 + 1) * P], AO[:, t, c * P:(c + 1) * P],
                                           identf[:])
                    ins.then_inc(S["aot_tr"], 1)
            pe.wait_ge(S["in_proj"], 16)
            for t in range(NT):
                pe.wait_ge(S["aot_evac"], 4 if t < 4 else 8)
                for k in range(DC):
                    ins = mm(ps[:, t, :], AOT[:, k, tile(t)], wproj[:, k, :], start=(k == 0), stop=(k == DC - 1))
                ins.then_inc(S["pj_mm"], 1)
            pe.wait_ge(S["pj_y"], NT // 2)
            ln_transpose(3, 0)
            pe.wait_ge(S["in_gu"], 32)
            for i in range(2 * IC):
                if i == 1:
                    pe.wait_ge(S["pj_y"], NT)
                    ln_transpose(3, 1)
                h, ib, s = i // IC, i % IC, i % 2
                M = M_of(i)
                pe.wait_ge(S["ln_hT"], 28 + 4 * h)
                if i >= 2:
                    pe.wait_ge(S["f_y0"], i - 1)
                for b, w in ((0, wg), (1, wu)):
                    for k in range(DC):
                        ins = mm(ps[0:M, 2 * s + b, :], w[:, k, ib * P:ib * P + M], hT[:, k, half(h)],
                                 start=(k == 0), stop=(k == DC - 1))
                ins.then_inc(S["g_mm"], 1)
            pe.wait_ge(S["wd_p2"], IC)
            for t in range(NT):
                pe.wait_ge(S["f_out"], IC * (t // 4 + 1))
                if t >= 4:
                    pe.wait_ge(S["dn_y"], t - 3)
                for k in range(IC):
                    M = M_of(k)
                    for part in range(3):
                        ins = mm(ps[:, 4 + t % 4, :], inter[0:M, k, tile(t)], wdp[0:M, part, k, :],
                                 start=(k == 0 and part == 0), stop=(k == IC - 1 and part == 2))
                ins.then_inc(S["dn_mm"], 1)

        @block.vector
        def _(v):
            n = [0]

            def link(ins):
                n[0] += 1
                ins.then_inc(S["dchain"], 1)
                v.wait_ge(S["dchain"], n[0])

            ts, tt, stt = v.tensor_scalar, v.tensor_tensor, v.scalar_tensor_tensor

            def ln_stats(tiles):
                for t in tiles:
                    v.bn_stats(stats[:, t, :], x_tok[:, t, :]).then_inc(S["dchain"], 1)
                    n[0] += 1

            def ln_var(h):
                v.wait_ge(S["dchain"], n[0])
                for t in range(4 * h, 4 * h + 4):
                    v.bn_aggr(mv[:, t, :], stats[:, t, :]).then_inc(S["dchain"], 1)
                    n[0] += 1
                v.wait_ge(S["dchain"], n[0])
                ts(veps[:, 4 * h:4 * h + 4], mv[:, 4 * h:4 * h + 4, 1], EPS, None, ALU.add).then_inc(S["ln_ve"], 1)

            def ln_norm(l, h):
                v.wait_ge(S["ln_rstd"], 2 * l + h + 1)
                for t in range(4 * h, 4 * h + 4):
                    if not (l == 0 and t < 2):
                        v.wait_ge(S["ln_tr"], NT * l + t - 1)
                    ts(xn[:, t % 2, :], x_tok[:, t, :], mv[:, t, 0:1], rstd[:, t:t + 1], ALU.subtract, ALU.mult) \
                        .then_inc(S["ln_norm"], 1)

            def mod_sum(layer):
                v.wait_ge(in_wm[layer][0], 16)
                link(ts(wmod[:, 0, :], wmod[:, 0, :], sc[:, layer, 0:1], None, ALU.mult))
                for k in range(1, DC):
                    v.wait_ge(in_wm[layer][k], 16)
                    ins = stt(wmod[:, 0, :], wmod[:, k, :], sc[:, layer, k:k + 1], wmod[:, 0, :], ALU.mult, ALU.add)
                    if k < DC - 1:
                        link(ins)
                ins.then_inc(S["mod_acc"], 1)

            def gate(dst, src, tmp):
                link(ts(tmp, src, 0.0, 2.0, ALU.is_ge, ALU.mult))
                link(stt(dst, tmp, 1.0, src, ALU.subtract, ALU.mult))
                link(ts(dst, dst, 0.25, None, ALU.max))
                link(stt(dst, tmp, 1.0, dst, ALU.subtract, ALU.mult))

            v.wait_ge(S["in_c"], 16)
            v.wait_ge(S["c_exp"], 1)
            link(ts(ce[:], ce[:], 1.0, None, ALU.add))
            link(v.reciprocal(ce[:], ce[:]))
            link(tt(sc[:], cc[:], ce[:], ALU.mult))
            v.wait_ge(S["in_x"], 16)
            ln_stats(range(0, 4))
            ln_var(0)
            ln_norm(0, 0)
            ln_stats(range(4, NT))
            ln_var(1)
            mod_sum(0)
            v.wait_ge(S["mod_mm"], 1)
            link(v.tensor_copy(modc[:, 0, 0:2, :], ps[:, 6, 0:8].rearrange("p (j c) -> p j c", c=DC)))
            ts(modc[:, 0, 1, :], modc[:, 0, 1, :], 1.0, None, ALU.add).then_inc(S["mod_done"], 1)
            ln_norm(0, 1)
            for h in range(2):
                v.wait_ge(S["xp_mm"], h + 1)
                link(v.tensor_copy(dtin[:, half(h)], ps[0:RANK, 4 * h, :]))
                v.tensor_copy(bcf[:, half(h)], ps[32:64, 4 * h, :]).then_inc(S["xp_dt"], 1)
            v.wait_ge(S["negA"], 1)
            v.wait_ge(S["in_misc"], 16 * 6)
            link(ts(bqk[:, 0:4], bqk[:, 0:4], 1.0 / HD, None, ALU.mult))
            ts(nA[:], nA[:], -1.0, None, ALU.mult).then_inc(S["negA"], 1)

            def split_bc(h):
                b, m_ = bcf[:, half(h)], mid[:, half(h)]
                v.wait_ge(S["xp_dt"], h + 1)
                link(v.tensor_copy(BCs[0:32, half(h)], b))
                link(tt(b, b, BCs[0:32, half(h)], ALU.subtract))
                link(v.tensor_copy(m_, b))
                link(v.tensor_copy(BCs[32:64, half(h)], m_))
                link(tt(b, b, m_, ALU.subtract))
                v.tensor_copy(BCs[64:96, half(h)], b).then_inc(S["xp_bc"], 1)

            for h in range(2):
                for c in range(DC):
                    v.wait_ge(S["sp_e"], DC * h + c + 1)
                    ts(sp_w[:, c, :], sp_exp[:, c, :], 1.0, None, ALU.add).then_inc(S["sp_w"], 1)
                split_bc(h)
                for c in range(DC):
                    ts(dtT[:, c, half(h)], ps[:, 4 * h + c, :], dtb[:, c:c + 1], 0.0, ALU.add, ALU.max)
                    v.wait_ge(S["sp_act"], DC * h + c + 1)
                    link(stt(sp_w[:, c, :], sp_w[:, c, :], 1.0, sp_exp[:, c, :], ALU.subtract, ALU.subtract))
                    link(tt(sp_log[:, c, :], sp_log[:, c, :], sp_w[:, c, :], ALU.subtract))
                    v.wait_ge(S["sp_lo"], DC * h + c + 1)
                    link(tt(sp_log[:, c, :], sp_log[:, c, :], uT[:, c, half(h)], ALU.max))
                    tt(sp_log[:, c, :], sp_log[:, c, :], sp_exp[:, c, :], ALU.min).then_inc(S["sp_dve"], 1)
            v.wait_ge(S["mod_mm"], 2)
            link(v.tensor_copy(modc[:, 0, 2:5, :], ps[:, 0, 8:20].rearrange("p (j c) -> p j c", c=DC)))
            gate(gb0[:], ps[:, 1, :], wrk[:])
            link(v.tensor_copy(modt[:, 0, :], modc[:, 0, 2, :]))
            gate(modc[:, 0, 2, :], modt[:, 0, :], modt[:, 1, :])
            ts(modc[:, 0, 4, :], modc[:, 0, 4, :], 1.0, None, ALU.add).then_inc(S["mod_rest"], 1)
            v.wait_ge(S["sp_free"], 2 * DC)
            v.wait_ge(S["setup"], 3)

            def scan(h, m, first_, last):
                def contribution(o, c):
                    N = m * 2 + (16 * h + o)
                    v.wait_ge(S["scan_done"], N * DC + (c + 1))
                    if h == 0:
                        v.tensor_copy(state[:, bass.ds(m * 2 + (o + c * NS), 1)], hs[:, c % 2, HALF - 1:HALF]) \
                            .then_inc(S["st_done"], 1)
                    v.wait_ge(S["c_mm"], N + 1)
                    if not (first_ and o == 0 and c < 2):
                        v.wait_ge(S["sum_done"], N * DC + (c - 1))
                    tt(hC[:, c % 2, :], hs[:, c % 2, :], ps[:, 4 + o, :], ALU.mult).then_inc(S["hc_done"], 1)

                before = None
                for o in range(2):
                    N = m * 2 + (16 * h + o)
                    for c in range(DC):
                        v.wait_ge(S["da_done"], N * DC + (c + 1))
                        v.wait_ge(S["dbx_done"], N * DC + (c + 1))
                        if not (first_ and o == 0 and c < 2):
                            v.wait_ge(S["hc_done"], N * DC + (c - 1))
                        init = 0.0 if h == 0 else state[:, bass.ds(m * 2 + (o + c * NS), 1)]
                        v.tensor_tensor_scan(hs[:, c % 2, :], dA[:, c, :], dBx[:, c, :], init, ALU.mult, ALU.add) \
                            .then_inc(S["scan_done"], 1)
                        if before:
                            contribution(*before)
                        before = (o, c)
                contribution(*before)
                if last:
                    v.wait_ge(S["y_done"], h + 1)
                    for c in range(DC):
                        link(stt(dtT[:, c, half(h)], hT[:, c, half(h)], Dp[:, c:c + 1], ps[:, c, :], ALU.mult, ALU.add))
                        ts(dtT[:, c, half(h)], dtT[:, c, half(h)], modc[:, 0, 2, c:c + 1], None, ALU.mult) \
                            .then_inc(S["ym"], 1)
                    for t in range(4):
                        v.wait_ge(S["yt"], 4 * h + t + 1)
                        tt(x_tok[:, 4 * h + t, :], x_tok[:, 4 * h + t, :], ps[:, t, :], ALU.add).then_inc(S["x0"], 1)
                    for t in range(4 * h, 4 * h + 4):
                        v.wait_ge(S["x0"], t + 1)
                        ln_stats((t,))
                    ln_var(h)
                    if h == 0:
                        v.wait_ge(S["st_done"], DC * NS)

            scan_turns(v, scan)
            v.wait_ge(S["x0"], NT)
            ln_norm(1, 0)
            ln_norm(1, 1)
            v.wait_ge(S["bias0"], 16 * 5)
            tt(bbc[:], bbc[:], gb0[:], ALU.mult).then_inc(S["bias0"], 1)
            link(v.tensor_copy(emapf[:], emapi[:]))
            link(tt(onehot[:], eidx[:], emapf[:].unsqueeze(1).to_broadcast([P, E, NR]), ALU.is_equal))
            for b in range(4):
                v.wait_ge(S["ar_mm"], 2 * b + 2)
                link(tt(lgt[:, 2 * b:2 * b + 2, :],
                        ps[:, b, :].rearrange("p (t c) -> p t c", t=2)[:, :, E * R:E * R + NR],
                        rb[:].unsqueeze(1).to_broadcast([P, 2, NR]), ALU.add))
            mx, sm = rsum8[:, 0, :], rsum8[:, 1, :]
            link(v.reduce_max(mx, lgt[:], AX))
            tt(lgt[:], lgt[:], mx.unsqueeze(2).to_broadcast([P, NT, NR]), ALU.subtract).then_inc(S["r_soft"], 1)
            v.wait_ge(S["r_exp"], 1)
            link(v.reduce_sum(sm, prb[:], AX))
            link(v.reciprocal(sm, sm))
            link(tt(prb[:], prb[:], sm.unsqueeze(2).to_broadcast([P, NT, NR]), ALU.mult))
            for t in range(NT):
                pj = prb[:, t, :].unsqueeze(1).to_broadcast([P, NR, NR])
                pi = prb[:, t, :].unsqueeze(2).to_broadcast([P, NR, NR])
                tt(cmpg[:, t], pj, pi, ALU.is_gt).then_inc(S["dchain"], 1)
                tt(cmpe[:, t], pj, pi, ALU.is_equal).then_inc(S["dchain"], 1)
                n[0] += 2
            v.wait_ge(S["dchain"], n[0])
            low = lower[:].rearrange("p i j -> p (i j)").unsqueeze(1).to_broadcast([P, NT, NR * NR])
            flat = lambda x: x[:].rearrange("p t i j -> p t (i j)")
            link(tt(flat(cmpe), flat(cmpe), low, ALU.mult))
            link(tt(flat(cmpg), flat(cmpg), flat(cmpe), ALU.add))
            link(v.reduce_sum(rank[:], cmpg[:], AX))
            link(stt(prb[:], rank[:], float(E), prb[:], ALU.is_lt, ALU.mult))
            link(ts(prb[:], prb[:], 2.0, None, ALU.mult))
            prod = cmpg[:].rearrange("p t i j -> p (t i j)")[:, 0:NT * E * NR]
            for t in range(NT):
                tt(prod[:, t * E * NR:(t + 1) * E * NR].rearrange("p (e i) -> p e i", e=E), onehot[:],
                   prb[:, t, :].unsqueeze(1).to_broadcast([P, E, NR]), ALU.mult).then_inc(S["dchain"], 1)
                n[0] += 1
            v.wait_ge(S["dchain"], n[0])
            link(v.reduce_sum(wexp[:].rearrange("p t e -> p (t e)"), prod.rearrange("p (k i) -> p k i", i=NR), AX))
            for b in range(4):
                ins = tt(hw[:, 2 * b:2 * b + 2, :].rearrange("p t (e r) -> p t e r", r=R),
                         ps[:, b, :].rearrange("p (t c) -> p t c", t=2)[:, :, 0:E * R]
                         .rearrange("p t (e r) -> p t e r", r=R),
                         wexp[:, 2 * b:2 * b + 2, :].unsqueeze(3).to_broadcast([P, 2, E, R]), ALU.mult)
                if b < 3:
                    link(ins)
            ins.then_inc(S["hw_done"], 1)

            def gated(mmsem, ysem, xsem, presem, bank, g, halfway=None):
                for t in range(NT + 2):
                    if t == NT // 2 and halfway:
                        halfway()
                    if t < NT:
                        v.wait_ge(S[mmsem], t + 1)
                        if t >= 2:
                            v.wait_ge(S[xsem], t - 1)
                        tt(yst[:, t % 2, :], ps[:, bank(t), :], g[:], ALU.mult).then_inc(S[ysem], 1)
                    if 1 <= t <= NT:
                        v.wait_ge(S[ysem], t)
                        v.wait_ge(S[presem], t)
                        tt(x_tok[:, t - 1, :], x_tok[:, t - 1, :], yst[:, (t - 1) % 2, :], ALU.add) \
                            .then_inc(S[xsem], 1)
                    if t >= 2:
                        v.wait_ge(S[xsem], t - 1)
                        ln_stats((t - 2,))
                        if t - 2 in (NT // 2 - 1, NT - 1):
                            ln_var((t - 2) // 4)

            def layer1_mods():
                v.wait_ge(S["mod_mm"], 3)
                pm = ps[:, 1, 0:24].rearrange("p (j c) -> p j c", c=DC)
                link(v.tensor_copy(modc[:, 1, 0:2, :], pm[:, 0:2, :]))
                link(v.tensor_copy(modc[:, 1, 3:5, :], pm[:, 3:5, :]))
                gate(ga1[:], ps[:, 2, :], wrk[:])
                gate(gb1[:], ps[:, 3, :], wrk[:])
                link(ts(modc[:, 1, 1, :], modc[:, 1, 1, :], 1.0, None, ALU.add))
                link(ts(modc[:, 1, 4, :], modc[:, 1, 4, :], 1.0, 1.0 / 128.0, ALU.add, ALU.mult))
                ts(modc[:, 1, 3, :], modc[:, 1, 3, :], 1.0 / 128.0, None, ALU.mult).then_inc(S["mod_done"], 1)

            gated("f0_mm", "f0_y", "x1", "x1pre", lambda t: 4 + t % 4, gb0, layer1_mods)
            ln_norm(2, 0)
            ln_norm(2, 1)
            v.wait_ge(S["bias1"], 32)
            tt(bpc[:], bpc[:], ga1[:], ALU.mult).then_inc(S["bias1"], 1)
            for i in range(16):
                s, s3 = i % 2, i % 3
                v.wait_ge(S["qk_evac"], i + 1)
                if i >= 3:
                    v.wait_ge(qk_wr[s3], 48 * (i // 3))
                link(v.tensor_copy(qkp[:, s3, 0, :], qkf[:, s, :]))
                link(tt(qkf[:, s, :], qkf[:, s, :], qkp[:, s3, 0, :], ALU.subtract))
                link(v.tensor_copy(qkp[:, s3, 1, :], qkf[:, s, :]))
                tt(qkp[:, s3, 2, :], qkf[:, s, :], qkp[:, s3, 1, :], ALU.subtract).then_inc(S["qk_split"], 1)
            link(v.memset(mrow[:], LOW))

            def value(t):
                v.wait_ge(S["v_mm"], t + 1)
                tt(V[:, t, :], ps[:, 4 + t % 4, :], vbc[:], ALU.add).then_inc(S["v_done"], 1)

            def maxima(g, s, values=False):
                t = V_FIRST
                if values:
                    for t_ in range(V_FIRST):
                        value(t_)
                for p in range(NPG):
                    j, (i, k0, w) = p // NP1, SPIECES[p % NP1]
                    v.wait_ge(S["s_mm"], g * NPG + (p + 1))
                    v.reduce_max(mrow[:, k0 // 512, j, i:i + 1], ps[:, p % 2, 0:w], AX).then_inc(S["m_done"], 1)
                    if values and p + 1 == score_pieces(t, DC - 1):
                        value(t)
                        t += 1
                v.wait_ge(S["m_done"], g * NPG + NPG)
                flat_m = mrow[:].rearrange("p a j i -> p a (j i)")
                if not first(g):
                    v.wait_ge(S["rt_mm"], g)
                tt(rr[:], flat_m[:, 0, :], flat_m[:, 1, :], ALU.max).then_inc(S["rr_max"], 1)
                v.wait_ge(S["rr_max"], g + 1)
                ts(rr[:], rr[:], -1.0, None, ALU.mult) \
                    .then_inc(S["r_rdy"], 1)
                v.wait_ge(S["rt_mm"], g + 1)
                if not first(g):
                    v.wait_ge(rrow[1 - s], (g - 1 - (1 - s)) * 24 + 48)
                pr = ps[0:GH * NT, 0, 0:P]
                v.tensor_copy(r3[:, 0, :], pr).then_inc(S["r_part"], 1)
                v.wait_ge(S["r_part"], g * 3 + 1)
                tt(rd[:], pr, r3[:, 0, :], ALU.subtract).then_inc(S["r_part"], 1)
                v.wait_ge(S["r_part"], g * 3 + 2)
                v.tensor_copy(r3[:, 1, :], rd[:]).then_inc(S["r_part"], 1)
                v.wait_ge(S["r_part"], g * 3 + 3)
                tt(r3[:, 2, :], rd[:], r3[:, 1, :], ALU.subtract).then_inc(S["rt_evac"], 1)

            maxima(0, 0, True)

            def attention(g, s, last):
                if not last:
                    maxima(g + 1, 1 - s)
                for b in range(2):
                    v.wait_ge(S["ot_tr"], g * 2 + (b + 1))
                    o = ps[:, 1 - b, :].rearrange("p (t j d) -> p t j d", t=4, d=32)
                    v.reciprocal(rec[:, b, :, :], o[:, :, :, HD]).then_inc(S["rec_done"], 1)
                    v.wait_ge(S["rec_done"], g * 2 + (b + 1))
                    tt(AO[:, 4 * b:4 * b + 4, bass.ds(g * (GH * HD), GH * HD)].rearrange("p t (j d) -> p t j d", d=HD),
                       o[:, :, :, 0:HD], rec[:, b, :, :].unsqueeze(3).to_broadcast([P, 4, GH, HD]), ALU.mult) \
                        .then_inc(S["ao_done"], 1)

            groups(v, attention)
            gated("pj_mm", "pj_y", "x2", "x2pre", lambda t: t, ga1)
            ln_norm(3, 0)
            ln_norm(3, 1)

            def trunc(y, s, M, sgn_sem, sgn_count, dst):
                link(ts(f_a[0:M, s, :].bitcast(I32), y.bitcast(I32), 0x7FFFFFFF, None, ALU.bitwise_and))
                link(ts(f_m[0:M, s, :], f_a[0:M, s, :], MAGIC, None, ALU.add))
                link(stt(f_a[0:M, s, :], f_m[0:M, s, :], MAGIC, f_a[0:M, s, :], ALU.subtract, ALU.subtract))
                link(stt(f_m[0:M, s, :], f_a[0:M, s, :], 0.0, f_m[0:M, s, :], ALU.is_gt, ALU.subtract))
                v.wait_ge(sgn_sem, sgn_count)
                return stt(dst, f_m[0:M, s, :], MAGIC, f_s[0:M, s, :], ALU.add, ALU.mult)

            for i in range(2 * IC):
                h, ib, s = i // IC, i % IC, i % 2
                M = M_of(i)
                v.wait_ge(S["f_exp"], i + 1)
                link(stt(f_r[0:M, s, :], ps[0:M, 2 * s, :], 128.0, f_e[0:M, s, :], ALU.mult, ALU.mult))
                if i >= 2:
                    v.wait_ge(S["f_sgn"], i - 1)
                link(tt(f_y[0:M, s, :], f_r[0:M, s, :], ps[0:M, 2 * s + 1, :], ALU.mult))
                ts(f_y[0:M, s, :], f_y[0:M, s, :], -128.0, 127.0, ALU.max, ALU.min).then_inc(S["f_y0"], 1)
                v.wait_ge(S["f_y0"], i + 1)
                trunc(f_y[0:M, s, :], s, M, S["f_sgn"], i + 1, inter[0:M, ib, half(h)]).then_inc(S["f_out"], 1)
            for t in range(NT):
                s = t % 2
                v.wait_ge(S["dn_mm"], t + 1)
                link(ts(f_y[:, s, :], ps[:, 4 + t % 4, :], -128.0, -128.0, ALU.mult, ALU.max))
                ts(f_y[:, s, :], f_y[:, s, :], 127.0, None, ALU.min).then_inc(S["dn_y0"], 1)
                v.wait_ge(S["dn_y0"], t + 1)
                link(trunc(f_y[:, s, :], s, P, S["dn_sgn"], t + 1, f_r[:, s, :]))
                tt(f_r[:, s, :], f_r[:, s, :], gb1[:], ALU.mult).then_inc(S["dn_y"], 1)
                v.wait_ge(S["dn_y"], t + 1)
                tt(x_tok[:, t, :], x_tok[:, t, :], f_r[:, s, :], ALU.subtract).then_inc(S["dn_done"], 1)


def bf16_bits(x):
    b = np.ascontiguousarray(x, dtype=np.float32).view(np.uint32)
    return ((b + 0x7FFF + ((b >> 16) & 1)) >> 16).astype(np.uint16)


def bf16_value(b):
    return (b.astype(np.uint32) << 16).view(np.float32)


def alibi_slopes():
    cp2 = 2 ** math.floor(math.log2(NH))
    b = 2 ** (-2 ** (-(math.log2(cp2) - 3)))
    return (b ** np.arange(1, cp2 + 1, dtype=np.float32)).astype(np.float32)


def constants():

    def three(x):
        h = bf16_bits(x)
        m = bf16_bits(x - bf16_value(h))
        return h, m, bf16_bits(x - bf16_value(h) - bf16_value(m))

    sl = alibi_slopes()
    p = np.arange(P)
    j = np.arange(T)
    qconst = np.zeros((ATT_A, T), np.float32)
    alibi = np.zeros((NH, ATT_A, T), np.uint16)
    for b in range(NT):
        qconst[3 * b:3 * b + 3, b * P:(b + 1) * P] = 1.0
        for n, part in enumerate(three(sl[:, None] * (j - (b * P + 64)).astype(np.float32)[None, :])):
            alibi[:, 3 * b + n, :] = part
    return {
        "ident": np.eye(P, dtype=np.float32), "identb": bf16_bits(np.eye(P)),
        "sel": bf16_bits(np.tile(np.eye(2 * NS), (3, 1))),
        "negm": bf16_bits(np.where(p[:, None] > p[None, :], -1e38, 0.0)),
        "qconst": bf16_bits(qconst), "kones": bf16_bits(np.ones((ATT_R, T))), "alibi": alibi,
        "lower": np.tile(np.tril(np.ones((NR, NR), np.float32), -1)[None], (P, 1, 1)),
        "eidx": np.tile(np.arange(E, dtype=np.float32)[None, :, None], (P, 1, NR)),
    }


def kernel(**inp):
    from concourse import bacc
    from concourse.bass_utils import run_bass_kernel_spmd

    c = np.ascontiguousarray
    g = {k: np.asarray(x) for k, x in inp.items()}
    cols = lambda x: c(x.reshape(-1, P).T)
    xp = g["L0_attn_x_proj_w"]
    xpw = np.zeros((D, 64), np.float32)
    xpw[:, 0:RANK] = xp[0:RANK].T
    xpw[:, 32:64] = xp[RANK:].T
    b_attn = g["L1_attn_b_attn"]
    arrays = dict(
        x=c(g["L0_attn_x"].reshape(NT, P, D).transpose(1, 0, 2)),
        c=c(np.stack([cols(g["L0_c"][0]), cols(g["L1_c"][0])], axis=1)),
        wmod0=c(g["L0_wmod"]), wmod1=c(g["L1_wmod"]),
        A_log=c(g["L0_attn_A_log"].reshape(DC, P, NS).transpose(1, 0, 2).reshape(P, DC * NS)),
        D=cols(g["L0_attn_D"]), dt_b=cols(g["L0_attn_dt_proj_b"]),
        xpw=xpw, dtw=c(g["L0_attn_dt_proj_w"].T),
        wbase=c(g["L0_ffn_base_W"].T), base_b=c(g["L0_ffn_base_b"]),
        war=c(np.concatenate([g["L0_ffn_A"].reshape(E * R, D), g["L0_ffn_router_W"]], axis=0).T),
        router_b=c(g["L0_ffn_router_b"]), emap=c(g["L0_ffn_expert_map"]),
        wlb=c(g["L0_ffn_B"].transpose(0, 2, 1).reshape(E * R, D)),
        wattn=c(g["L1_attn_w_attn"]), b_qk=cols(b_attn[0:2 * D]), b_v=c(b_attn[2 * D:]),
        wproj=c(g["L1_attn_w_proj"]), b_proj=c(g["L1_attn_b_proj"]),
        wg=c(g["L1_ffn_w_gate"].T), wu=c(g["L1_ffn_w_up"].T), wd=c(g["L1_ffn_w_down"].T),
        **constants(),
    )
    nc = bacc.Bacc("TRN2", target_bir_lowering=False, num_devices=1)
    aps = {k: nc.dram_tensor(f"in_{k}", x.shape, mybir.dt.from_np(x.dtype), kind="ExternalInput").ap()
           for k, x in arrays.items()}
    out = nc.dram_tensor("out_x", (T, D), F32, kind="ExternalOutput").ap()
    program(nc, aps, out)
    r = run_bass_kernel_spmd(nc, [{f"in_{k}": x for k, x in arrays.items()}], core_ids=[0])
    return r.results[0]["out_x"].reshape(1, T, D)
```
